# Optimizing a Trainium2 kernel written in Bass

```python
import numpy as np
import jax
import jax.numpy as jnp

def _softmax(x, axis=-1):
    return jax.nn.softmax(x, axis=axis)

def _gelu(x):
    return jax.nn.gelu(x, approximate=True)

def _silu(x):
    return jax.nn.silu(x)

def _sigmoid(x):
    return jax.nn.sigmoid(x)

def _layernorm(x, axis=-1, eps=1e-05):
    m = jnp.mean(x, axis=axis, keepdims=True)
    v = jnp.var(x, axis=axis, keepdims=True)
    return (x - m) / jnp.sqrt(v + eps)

def _scatter_add(tgt, idx, src, axis=0):
    return tgt.at[idx].add(src)

def _segment_sum(src, seg, n):
    return jax.ops.segment_sum(src, seg, n)
kernel_name = 'mk_macaron_d1_jaxref_r8_278a5f'

def setup_inputs(seed: int=0):
    np.random.seed(seed)
    _w = jnp.asarray

    def _L0_attn_setup():
        import jax, jax.numpy as jnp
        import numpy as np
        B, S, D = (4, 256, 128)
        key = jax.random.key(seed)
        k1, k2, k3, k4 = jax.random.split(key, 4)
        x = jax.random.normal(k1, (B, S, D), dtype=jnp.float32)
        Qw = jax.random.normal(k2, (D, D), dtype=jnp.float32) / 40
        Kw = jax.random.normal(k3, (D, D), dtype=jnp.float32) / 40
        Vw = jax.random.normal(k4, (D, D), dtype=jnp.float32) / 40
        return {'x': x, 'Qw': Qw, 'Kw': Kw, 'Vw': Vw}
    _L0_attn_in = _L0_attn_setup()

    def _L0_ffn_setup():
        import jax, jax.numpy as jnp
        import numpy as np
        B, T, D = (2, 256, 128)
        DCD = 512
        RET = 128
        NEXP = 512
        NKEYS = 64
        H = 4
        KPH = 8
        key = jax.random.key(seed)
        ks = jax.random.split(key, 10)
        s = lambda k, shape, scale: jax.random.normal(k, shape, jnp.float32) * scale
        return {'hidden_states': jax.random.normal(ks[0], (B, T, D), jnp.float32), 'Wg': s(ks[1], (D, DCD), 0.02), 'bg': jnp.zeros((DCD,), jnp.float32), 'Wu': s(ks[2], (D, DCD), 0.02), 'bu': jnp.zeros((DCD,), jnp.float32), 'Wd': s(ks[3], (DCD, D), 0.02), 'bd': jnp.zeros((D,), jnp.float32), 'Wq': s(ks[4], (D, RET * H), 0.02), 'keys': s(ks[5], (H, NKEYS, 2, RET // 2), 0.02), 'down_embed': s(ks[6], (NEXP, D), 0.02), 'up_embed': s(ks[7], (NEXP, D), 0.02)}
    _L0_ffn_in = _L0_ffn_setup()
    _d = {'L0_attn_x': _L0_attn_in['x'], 'L0_attn_Qw': _L0_attn_in['Qw'], 'L0_attn_Kw': _L0_attn_in['Kw'], 'L0_attn_Vw': _L0_attn_in['Vw'], 'L0_ffn_Wg': _L0_ffn_in['Wg'], 'L0_ffn_bg': _L0_ffn_in['bg'], 'L0_ffn_Wu': _L0_ffn_in['Wu'], 'L0_ffn_bu': _L0_ffn_in['bu'], 'L0_ffn_Wd': _L0_ffn_in['Wd'], 'L0_ffn_bd': _L0_ffn_in['bd'], 'L0_ffn_Wq': _L0_ffn_in['Wq'], 'L0_ffn_keys': _L0_ffn_in['keys'], 'L0_ffn_down_embed': _L0_ffn_in['down_embed'], 'L0_ffn_up_embed': _L0_ffn_in['up_embed']}
    _x0 = _d['L0_attn_x']
    _d['L0_attn_x'] = jax.random.normal(jax.random.fold_in(jax.random.key(seed), 1), (8, 256, 128), dtype=_x0.dtype)
    del _x0
    return _d

def reference(L0_attn_x, L0_attn_Qw, L0_attn_Kw, L0_attn_Vw, L0_ffn_Wg, L0_ffn_bg, L0_ffn_Wu, L0_ffn_bu, L0_ffn_Wd, L0_ffn_bd, L0_ffn_Wq, L0_ffn_keys, L0_ffn_down_embed, L0_ffn_up_embed):

    def _L0_attn_ref(x, Qw, Kw, Vw):
        import jax, jax.numpy as jnp
        import numpy as np
        B, S, D = (4, 256, 128)
        Q = x @ Qw
        K = x @ Kw
        V = x @ Vw
        d = x.shape[-1]
        S_len = x.shape[-2]
        mask = jnp.where(jnp.tril(jnp.ones((S_len, S_len), dtype=x.dtype)) == 0, -jnp.inf, 0.0).astype(x.dtype)
        scores = jnp.einsum('bqd,bkd->bqk', Q, K) / jnp.sqrt(jnp.asarray(d, x.dtype))
        scores = scores + mask
        attn = jax.nn.softmax(scores, axis=-1)
        return jnp.einsum('bqk,bkd->bqd', attn, V)

    def _L0_ffn_ref(hidden_states, Wg, bg, Wu, bu, Wd, bd, Wq, keys, down_embed, up_embed):
        import jax, jax.numpy as jnp
        import numpy as np
        B, T, D = (2, 256, 128)
        DCD = 512
        RET = 128
        NEXP = 512
        NKEYS = 64
        H = 4
        KPH = 8
        b, t, d = hidden_states.shape
        q = (hidden_states @ Wq).reshape(b, t, 2, H, RET // 2)
        sim = jnp.einsum('btphn,hkpn->pbthk', q, keys)
        sc, ix = jax.lax.top_k(sim, KPH)
        sx, sy = (sc[0], sc[1])
        ixx, ixy = (ix[0], ix[1])
        all_sc = (sx[..., :, None] + sy[..., None, :]).reshape(b, t, H, KPH * KPH)
        all_ix = (ixx[..., :, None] * NKEYS + ixy[..., None, :]).reshape(b, t, H, KPH * KPH)
        scores, pk = jax.lax.top_k(all_sc, KPH)
        idx = jnp.take_along_axis(all_ix, pk, axis=-1)
        de = down_embed[idx]
        ue = up_embed[idx]
        w = jnp.einsum('btd,bthkd->bthk', hidden_states, de)
        w = jax.nn.silu(w) * jax.nn.softmax(scores, axis=-1)
        experts_states = jnp.einsum('bthk,bthkd->btd', w, ue)
        mlp = jax.nn.silu(hidden_states @ Wg + bg) * (hidden_states @ Wu + bu) @ Wd + bd
        return mlp + experts_states
    x = L0_attn_x
    x = x + 0.5 * _L0_ffn_ref(_layernorm(x, axis=-1), L0_ffn_Wg, L0_ffn_bg, L0_ffn_Wu, L0_ffn_bu, L0_ffn_Wd, L0_ffn_bd, L0_ffn_Wq, L0_ffn_keys, L0_ffn_down_embed, L0_ffn_up_embed)
    x = x + _L0_attn_ref(_layernorm(x, axis=-1), L0_attn_Qw, L0_attn_Kw, L0_attn_Vw)
    x = x + 0.5 * _L0_ffn_ref(_layernorm(x, axis=-1), L0_ffn_Wg, L0_ffn_bg, L0_ffn_Wu, L0_ffn_bu, L0_ffn_Wd, L0_ffn_bd, L0_ffn_Wq, L0_ffn_keys, L0_ffn_down_embed, L0_ffn_up_embed)
    return x

_drawn_inputs = setup_inputs


def setup_inputs(seed=0):
    import zlib

    import numpy as np

    out = dict(_drawn_inputs(seed))
    spreads = {'L0_ffn_bg': (0.0, 0.8), 'L0_ffn_bu': (0.0, 0.8), 'L0_ffn_bd': (0.0, 0.1)}
    factors = {'L0_attn_Qw': 8.0,
     'L0_attn_Kw': 8.0,
     'L0_ffn_Wg': 4.388,
     'L0_ffn_Wu': 4.323,
     'L0_ffn_Wd': 3.937,
     'L0_ffn_Wq': 8.0,
     'L0_ffn_keys': 8.0,
     'L0_ffn_down_embed': 6.953,
     'L0_ffn_up_embed': 7.623}
    for name, (base, spread) in spreads.items():
        noise = np.random.default_rng([zlib.crc32(name.encode()), seed]).standard_normal(out[name].shape)
        drawn = base * np.exp(spread * noise) if base else spread * noise
        out[name] = jnp.asarray(drawn.astype(out[name].dtype))
    for name, factor in factors.items():
        out[name] = (out[name] * factor).astype(out[name].dtype)
    return out
```

```python
import numpy as np
import concourse.bass as bass
from concourse import mybir
from contextlib import ExitStack

B, S, D = 8, 256, 128
P = 128
NJ = S // P
F = 512
NE = 512
H, NK, NQ, TOP = 4, 64, 64, 8
NX = NE // NK
FC = F // P
G = NJ * H
NC = 24
EPS = 1e-5
SCALE = float(D) ** -0.5
NEG = -1e30


def build(nc, x_d, qw_d, kw_d, vw_d, wg_d, bg_d, wu_d, bu_d, wd_d, bd_d, wq_d, keys_d, down_d, up_d, out_d):
    f32 = mybir.dt.float32
    ALU = mybir.AluOpType
    ACT = mybir.ActivationFunctionType
    AX = mybir.AxisListType

    ctx = ExitStack()
    with ctx:
        def sb(name, shape):
            return ctx.enter_context(nc.sbuf_tensor(name, shape, f32))

        def sem(name):
            return ctx.enter_context(nc.semaphore(name))

        def sems(name, *dims):
            if not dims:
                return sem(name)
            return [sems(f"{name}_{k}", *dims[1:]) for k in range(dims[0])]

        wg = sb("wg", [P, F]); wu = sb("wu", [P, F]); wq = sb("wq", [P, 2 * H * NQ])
        wd = sb("wd", [P, FC, D]); up = sb("up", [P, FC, D]); down = sb("down", [P, FC, D])
        keys = sb("keys", [NK, H, 2 * NQ])
        qw = sb("qw", [P, D]); kw = sb("kw", [P, D]); vw = sb("vw", [P, D])
        brow = sb("brow", [2 * FC, P]); bias = sb("bias", [P, 2 * FC]); bd = sb("bd", [1, D])
        ident = sb("ident", [P, P])
        ones = sb("ones", [1, P])
        half = sb("half", [P, NJ])
        causal = sb("causal", [P, 3 * P])
        wqT = sb("wqT", [NQ, 2 * H, D])
        keyT = sb("keyT", [NQ, 2 * H, NK])
        qwT = sb("qwT", [P, D]); kwT = sb("kwT", [P, D])
        router = sb("router", [P, 2 * H * NK])
        qk = sb("qk", [P, D])
        downT = sb("downT", [P, NE])
        xin = sb("xin", [P, NJ, D])
        x1 = sb("x1", [P, NJ, D])
        x2 = sb("x2", [P, NJ, D])
        x3 = sb("x3", [P, NJ, D])
        LN1, LNA, LN2 = 0, 1, 2
        stats = sb("stats", [P, 3, NJ, 6])
        mv = sb("mv", [P, 3, NJ, 2])
        vare = sb("vare", [P, 3, NJ])
        rstd = sb("rstd", [P, 3, NJ])
        hn = sb("hn", [P, 3, NJ, D])
        hT = sb("hT", [P, 3, S])
        sims = sb("sims", [P, 2, NJ, 2, H * NK])
        best = sb("best", [P, 2, 2, G, TOP])
        cand = sb("cand", [P, 2, G, NC])
        top = sb("top", [P, 2, G, TOP])
        dtop = sb("dtop", [P, 2, G, TOP])
        etop = sb("etop", [P, 2, G, TOP])
        zsum = sb("zsum", [P, 2, G])
        lnz = sb("lnz", [P, 2, G])
        nbias = sb("nbias", [P, 2, G])
        gate = sb("gate", [P, 2, FC, S])
        upv = sb("upv", [P, 2, FC, S])
        act = sb("act", [P, 2, FC, S])
        sproj = sb("sproj", [P, 2, FC, S])
        pair = sb("pair", [P, NJ, H, NX * NK])
        prob = sb("prob", [P, NJ, H, NX * NK])
        dense = sb("dense", [P, NJ, NE])
        mass = sb("mass", [P, 2, NJ])
        wT = sb("wT", [P, NJ, FC, P])
        tv = sb("tv", [P, 2 * S])
        sc = sb("sc", [P, 3 * P])
        mx = sb("mx", [P, NJ]); nmx = sb("nmx", [P, NJ])
        pr = sb("pr", [P, 3 * P]); rs = sb("rs", [P, NJ]); rinv = sb("rinv", [P, NJ])
        prT = sb("prT", [P, 3 * P])

        bank = [ctx.enter_context(nc.psum_tensor(f"bank{i}", [P, 512], f32)) for i in range(8)]
        SIM, MLP, ST, Y, AUX = 0, 2, 5, 6, 7

        s_ld = {n: sem("ld_" + n) for n in ("wg", "wu", "wq", "wd", "up", "down", "keys", "qk", "vw", "b", "bd")}
        s_zero = sem("zeroed"); s_const = sem("constants")
        s_tr = sems("weights_transposed", 4)
        s_trc = sems("weights_transposed_copied", 4)
        s_fold = sems("weights_folded", 2)
        s_foldc = sems("weights_folded_copied", 2)
        s_x = sem("x_loaded"); s_out = sem("x3_stored")
        s_stat = sems("ln_stats", 3, NJ); s_mv = sems("ln_mean_var", 3); s_vare = sems("ln_var_eps", 3)
        s_rstd = sems("ln_rstd", 3); s_hn = sems("ln_normalised", 3); s_hTp = sems("ln_transposed", 3)
        s_hT = sems("ln_transposed_copied", 3)
        s_simp = sems("sims_multiplied", 2, NJ); s_sim = sems("sims_copied", 2, NJ)
        s_best = sems("side_best", 2); s_cand = sems("candidates", 2); s_top = sems("pair_best", 2)
        s_dtop = sems("top_shifted", 2); s_etop = sems("top_exp", 2); s_z = sems("softmax_sum", 2)
        s_lnz = sems("softmax_ln", 2); s_nb = sems("softmax_bias", 2)
        s_mlpp = sems("mlp_multiplied", 2, 6); s_mlp = sems("mlp_copied", 2, 6)
        s_act = sems("act_ready", 2)
        s_pair = sems("pair_sums", 2, NJ); s_exp = sems("pair_exp", 2, NJ); s_mask = sems("pair_masked", 2, NJ)
        s_add = sems("heads_added_once", 2, NJ); s_dense = sems("heads_added", 2, NJ); s_fix = sems("last_row", 2, NJ)
        s_sT = sems("dense_transposed", 2, NJ); s_wT = sems("weights_ready", 2, NJ)
        s_y = sems("ffn_multiplied", 2, NJ); s_res = sems("ffn_added", 2, NJ)
        s_tvp = sem("att_tv_multiplied"); s_tv = sem("att_tv_copied"); s_scp = sem("att_scores")
        s_sc = sem("att_masked"); s_mx = sem("att_max"); s_nmx = sem("att_bias"); s_pr = sem("att_probs")
        s_prTp = sem("att_probs_transposed"); s_prT = sem("att_probs_copied"); s_o = sem("att_out")
        s_rinv = sem("att_rinv"); s_x2 = sem("att_added")

        block = ctx.enter_context(nc.Block())

        def wait(eng, s, v):
            if not (isinstance(v, int) and v <= 0):
                eng.wait_ge(s, v)

        def steps(eng, step):
            step(2, 1, 0, True, False)
            with eng.Fori(1, B) as it:
                n = []
                for k in (2, 1):
                    reg = eng.alloc_register(f"step_plus_{k}")
                    eng.reg_add(reg, it, k)
                    n.append(eng.snap(reg, donate=True))
                step(n[0], n[1], it, True, True)
            step(B + 2, B + 1, B, False, True)

        def passes(n1, n0, first, second):
            out = []
            if first:
                out.append((0, n1, n0, 1, n0))
            if second:
                out.append((1, n1, n0, 0, n1) if first else (1, n1, n0, 1, n0))
            return out

        def skip_pass_1(eng, *lists):
            for s in lists:
                for x in s if isinstance(s, list) else [s]:
                    eng.sem_inc(x, 1)

        @block.sync
        def _(sp):
            for name, dst, src in (("wq", wq[:, :], wq_d), ("down", down[:, :, :], down_d.rearrange("(c p) d -> p c d", p=P)),
                                   ("wg", wg[:, :], wg_d), ("wu", wu[:, :], wu_d),
                                   ("up", up[:, :, :], up_d.rearrange("(c p) d -> p c d", p=P))):
                sp.dma_start(dst, src).then_inc(s_ld[name], 16)
            sp.dma_start(bd[:, :], bd_d.rearrange("(o d) -> o d", o=1)).then_inc(s_ld["bd"], 16)

            def store(b, count):
                for j in range(NJ):
                    sp.wait_ge(s_res[1][j], count)
                sp.dma_start(out_d[b].rearrange("(j p) d -> p j d", p=P), x3[:, :, :]).then_inc(s_out, 16)

            def load(b, count):
                for j in range(NJ):
                    sp.wait_ge(s_res[0][j], count)
                sp.dma_start(xin[:, :, :], x_d[b].rearrange("(j p) d -> p j d", p=P)).then_inc(s_x, 16)

            sp.sem_inc(s_out, 16)
            load(1, 1)
            with sp.Fori(1, B - 1) as it:
                load(it + 1, it + 1)
                store(it - 1, it + 1)
            load(B - 1, B)
            store(B - 2, B)
            store(B - 1, B + 1)
            sp.wait_ge(s_out, 16 * (B + 1))

        @block.gpsimd
        def _(pool):
            nc.gpsimd.memset(ident[:, :], 0.0).then_inc(s_zero, 1)
            nc.gpsimd.memset(causal[:, :], 0.0).then_inc(s_zero, 1)
            pool.wait_ge(s_zero, 2)
            nc.gpsimd.affine_select(out=ident[:, :], in_=ident[:, :], compare_op=ALU.not_equal, fill=1.0, base=0,
                                    pattern=[[-1, P]], channel_multiplier=1).then_inc(s_const, 1)
            for b in (0, 2):
                blk = causal[:, b * P:(b + 1) * P]
                nc.gpsimd.affine_select(out=blk, in_=blk, compare_op=ALU.is_ge, fill=NEG, base=0,
                                        pattern=[[-1, P]], channel_multiplier=1).then_inc(s_const, 1)
            nc.gpsimd.memset(half[:, :], -0.5).then_inc(s_const, 1)
            nc.gpsimd.memset(ones[:, :], 1.0).then_inc(s_const, 1)
            pool.wait_ge(s_const, 5)

            def power(ln, count):
                pool.wait_ge(s_vare[ln], count)
                nc.gpsimd.tensor_tensor(rstd[:, ln, :], vare[:, ln, :], half[:, :], ALU.pow).then_inc(s_rstd[ln], 1)

            power(LN1, 1)
            skip_pass_1(pool, s_pair[1], s_act[1])

            def product(s, cur, prev):
                wait(pool, s_y[s][NJ - 1], prev)
                for k in (0, 1, 4, 5):
                    pool.wait_ge(s_mlp[s][k], cur)
                nc.gpsimd.tensor_tensor(act[:, s], gate[:, s], upv[:, s], ALU.mult).then_inc(s_act[s], 1)

            def sums(s, cur, prev, o, left, j):
                pool.wait_ge(s_sim[s][j], cur)
                wait(pool, s_mask[o][j], left)
                simx = sims[:, s, j, 0].rearrange("p (h k) -> p h k", h=H)[:, :, 0:NX]
                simy = sims[:, s, j, 1].rearrange("p (h k) -> p h k", h=H)
                nc.gpsimd.tensor_tensor(pair[:, j].rearrange("p h (x y) -> p h x y", x=NX),
                                        simx.unsqueeze(3).to_broadcast([P, H, NX, NK]),
                                        simy.unsqueeze(2).to_broadcast([P, H, NX, NK]), ALU.add).then_inc(s_pair[s][j], 1)

            def step(n2, n1, n0, first, second):
                ps = passes(n1, n0, first, second)
                for s, cur, prev, o, left in ps[:1]:
                    sums(s, cur, prev, o, left, 0)
                    product(s, cur, prev)
                    sums(s, cur, prev, o, left, 1)
                for s, cur, prev, o, left in ps[1:]:
                    product(s, cur, prev)
                if first:
                    power(LNA, n1)
                for s, cur, prev, o, left in ps[1:]:
                    sums(s, cur, prev, o, left, 0)
                if first:
                    power(LN1, n2)
                for s, cur, prev, o, left in ps[1:]:
                    sums(s, cur, prev, o, left, 1)
                if first:
                    power(LN2, n1)

            steps(pool, step)

        @block.scalar
        def _(act_):
            act_.dma_start(xin[:, :, :], x_d[0].rearrange("(j p) d -> p j d", p=P)).then_inc(s_x, 16)
            act_.dma_start(keys[:, :, :], keys_d.rearrange("h k s n -> k h (s n)")).then_inc(s_ld["keys"], 16)
            act_.dma_start(qw[:, :], qw_d).then_inc(s_ld["qk"], 16)
            act_.dma_start(kw[:, :], kw_d).then_inc(s_ld["qk"], 16)
            act_.dma_start(brow[0:FC, :], bg_d.rearrange("(c p) -> c p", p=P)).then_inc(s_ld["b"], 16)
            act_.dma_start(brow[FC:2 * FC, :], bu_d.rearrange("(c p) -> c p", p=P)).then_inc(s_ld["b"], 16)
            act_.dma_start(vw[:, :], vw_d).then_inc(s_ld["vw"], 16)
            act_.dma_start(wd[:, :, :], wd_d.rearrange("(c p) d -> p c d", p=P)).then_inc(s_ld["wd"], 16)

            def copy_hT(ln, count):
                act_.wait_ge(s_hTp[ln], count)
                nc.scalar.copy(hT[:, ln], bank[AUX][:, 0:S]).then_inc(s_hT[ln], 1)

            copy_hT(LN1, 1)
            act_.wait_ge(s_tr[0], 1)
            nc.scalar.copy(wqT[:, 0:H].rearrange("p g d -> p (g d)"), bank[0][0:NQ, :]).then_inc(s_trc[0], 1)
            act_.wait_ge(s_tr[1], 1)
            nc.scalar.copy(wqT[:, H:2 * H].rearrange("p g d -> p (g d)"), bank[1][0:NQ, :]).then_inc(s_trc[0], 1)
            nc.scalar.copy(keyT[:, :, :].rearrange("p g k -> p (g k)"), bank[2][0:NQ, :]).then_inc(s_trc[0], 1)
            act_.wait_ge(s_tr[2], 1)
            nc.scalar.copy(downT[:, :], bank[3][:, :]).then_inc(s_trc[1], 1)
            act_.wait_ge(s_fold[0], 1)
            nc.scalar.copy(router[:, :], bank[4][:, :]).then_inc(s_foldc[0], 1)
            act_.wait_ge(s_tr[3], 1)
            nc.scalar.copy(qwT[:, :], bank[5][:, 0:D]).then_inc(s_trc[2], 1)
            nc.scalar.copy(kwT[:, :], bank[5][:, D:2 * D]).then_inc(s_trc[2], 1)
            nc.scalar.copy(bias[:, :], bank[5][:, 2 * D:2 * D + 2 * FC]).then_inc(s_trc[3], 1)
            act_.wait_ge(s_trc[3], 1)
            act_.wait_ge(s_fold[1], 1)
            nc.scalar.copy(qk[:, :], bank[6][:, 0:D]).then_inc(s_foldc[1], 1)

            def hidden(s, cur, prev):
                for j in range(NJ):
                    act_.wait_ge(s_simp[s][j], cur)
                    wait(act_, s_pair[s][j], prev)
                    wait(act_, s_best[s], prev)
                    nc.scalar.copy(sims[:, s, j].rearrange("p a k -> p (a k)"), bank[SIM + j][:, :]).then_inc(s_sim[s][j], 1)
                wait(act_, s_act[s], prev)
                for k in range(6):
                    act_.wait_ge(s_mlpp[s][k], cur)
                    b = bank[MLP + k % 3]
                    if k in (2, 3):
                        for j in range(NJ):
                            wait(act_, s_wT[s][j], prev)
                        c = 2 * (k - 2)
                        ins = nc.scalar.activation(sproj[:, s, c:c + 2].rearrange("p c t -> p (c t)"), b[:, :], ACT.Silu)
                    else:
                        dst, func, b0, c0 = (gate, ACT.Silu, 0, 2 * k) if k < 2 else (upv, ACT.Identity, FC, 2 * (k - 4))
                        for i in range(2):
                            ins = nc.scalar.activation(dst[:, s, c0 + i], b[:, i * S:(i + 1) * S], func,
                                                       bias=bias[:, b0 + c0 + i:b0 + c0 + i + 1])
                    ins.then_inc(s_mlp[s][k], 1)

            def normaliser(s, cur):
                act_.wait_ge(s_dtop[s], cur)
                nc.scalar.activation(etop[:, s], dtop[:, s], ACT.Exp).then_inc(s_etop[s], 1)
                act_.wait_ge(s_z[s], cur)
                nc.scalar.activation(lnz[:, s], zsum[:, s], ACT.Ln).then_inc(s_lnz[s], 1)

            def exps(s, cur, prev, o, left, j):
                act_.wait_ge(s_nb[s], cur)
                act_.wait_ge(s_pair[s][j], cur)
                wait(act_, s_dense[o][j], left)
                for h in range(H):
                    ins = nc.scalar.activation(prob[:, j, h], pair[:, j, h], ACT.Exp,
                                               bias=nbias[:, s, j * H + h:j * H + h + 1])
                ins.then_inc(s_exp[s][j], 1)

            def step(n2, n1, n0, first, second):
                ps = passes(n1, n0, first, second)
                for s, cur, prev, o, left in ps:
                    if s == 1:
                        copy_hT(LN2, cur)
                    hidden(s, cur, prev)
                for s, cur, prev, o, left in ps:
                    normaliser(s, cur)
                for j in range(NJ):
                    exps(*ps[0], j)
                for p_ in ps[1:]:
                    exps(*p_, 0)
                if first:
                    copy_hT(LNA, n1)
                    act_.wait_ge(s_tvp, n1)
                    nc.scalar.copy(tv[:, :], bank[AUX][:, :]).then_inc(s_tv, 1)
                if first:
                    act_.wait_ge(s_nmx, n1)
                    act_.wait_ge(s_sc, n1)
                    nc.scalar.activation(pr[:, 0:P], sc[:, 0:P], ACT.Exp, bias=nmx[:, 0:1], scale=SCALE,
                                         accum_out=rs[:, 0:1])
                    nc.scalar.activation(pr[:, P:3 * P], sc[:, P:3 * P], ACT.Exp, bias=nmx[:, 1:2], scale=SCALE,
                                         accum_out=rs[:, 1:2]).then_inc(s_pr, 1)
                for p_ in ps[1:]:
                    exps(*p_, 1)
                if first:
                    copy_hT(LN1, n2)
                    act_.wait_ge(s_prTp, n1)
                    nc.scalar.copy(prT[:, :], bank[AUX][:, 0:3 * P]).then_inc(s_prT, 1)

            skip_pass_1(act_, s_hT[LN2], s_sim[1], s_mlp[1], s_etop[1], s_lnz[1], s_exp[1])
            steps(act_, step)

        @block.vector
        def _(dve):
            src_of = {LN1: xin, LNA: x1, LN2: x2}

            def statistics(ln, count, j):
                nc.vector.bn_stats(stats[:, ln, j], src_of[ln][:, j]).then_inc(s_stat[ln][j], 1)

            def variance(ln, count, before):
                for j in range(NJ):
                    static_wait()
                    dve.wait_ge(s_stat[ln][j], count)
                    ins = nc.vector.bn_aggr(mv[:, ln, j], stats[:, ln, j])
                ins.then_inc(s_mv[ln], 1)
                dve.wait_ge(s_mv[ln], count)
                wait(dve, s_rstd[ln], before)
                nc.vector.tensor_scalar_add(vare[:, ln, :], mv[:, ln, :, 1], EPS).then_inc(s_vare[ln], 1)

            def normalise(ln, count, before):
                dve.wait_ge(s_rstd[ln], count)
                wait(dve, s_hTp[ln], before)
                for j in range(NJ):
                    ins = nc.vector.tensor_scalar(hn[:, ln, j], src_of[ln][:, j], mv[:, ln, j, 0:1],
                                                  rstd[:, ln, j:j + 1], ALU.subtract, ALU.mult)
                ins.then_inc(s_hn[ln], 1)

            def static_wait():
                dve.wait_ge(s_const, 5)

            dve.wait_ge(s_x, 16)
            for j in range(NJ):
                statistics(LN1, 1, j)
            variance(LN1, 1, 0)
            normalise(LN1, 1, 0)

            def search(s, cur):
                for j in range(NJ):
                    static_wait()
                    dve.wait_ge(s_sim[s][j], cur)
                    for side in range(2):
                        for h in range(H):
                            ins = nc.vector.max(best[:, s, side, j * H + h], sims[:, s, j, side, h * NK:(h + 1) * NK])
                ins.then_inc(s_best[s], 1)
                dve.wait_ge(s_best[s], cur)
                bx, by = best[:, s, 0], best[:, s, 1]
                nc.vector.tensor_tensor(cand[:, s, :, 0:8], bx[:, :, 0:1].to_broadcast([P, G, 8]), by, ALU.add)
                nc.vector.tensor_tensor(cand[:, s, :, 8:20].rearrange("p g (a b) -> p g a b", a=3),
                                        bx[:, :, 1:4].unsqueeze(3).to_broadcast([P, G, 3, 4]),
                                        by[:, :, 0:4].unsqueeze(2).to_broadcast([P, G, 3, 4]), ALU.add)
                nc.vector.tensor_tensor(cand[:, s, :, 20:24], bx[:, :, 4:8], by[:, :, 0:1].to_broadcast([P, G, 4]),
                                        ALU.add).then_inc(s_cand[s], 1)
                static_wait()
                dve.wait_ge(s_cand[s], cur)
                for g in range(G):
                    ins = nc.vector.max(top[:, s, g], cand[:, s, g])
                ins.then_inc(s_top[s], 1)
                dve.wait_ge(s_top[s], cur)
                nc.vector.tensor_tensor(dtop[:, s], top[:, s], top[:, s, :, 0:1].to_broadcast([P, G, TOP]),
                                        ALU.subtract).then_inc(s_dtop[s], 1)

            def softmax_sum(s, cur):
                dve.wait_ge(s_etop[s], cur)
                nc.vector.tensor_reduce(zsum[:, s], etop[:, s], AX.X, ALU.add).then_inc(s_z[s], 1)

            def softmax_bias(s, cur):
                dve.wait_ge(s_lnz[s], cur)
                nc.vector.scalar_tensor_tensor(out=nbias[:, s], in0=top[:, s, :, 0], scalar=-1.0, in1=lnz[:, s],
                                               op0=ALU.mult, op1=ALU.subtract).then_inc(s_nb[s], 1)

            def choose(s, cur, prev, o, left, j):
                dve.wait_ge(s_exp[s][j], cur)
                for h in range(H):
                    ins = nc.vector.scalar_tensor_tensor(out=prob[:, j, h], in0=pair[:, j, h],
                                                         scalar=top[:, s, j * H + h, TOP - 1:TOP], in1=prob[:, j, h],
                                                         op0=ALU.is_ge, op1=ALU.mult)
                ins.then_inc(s_mask[s][j], 1)
                dve.wait_ge(s_mask[s][j], cur)
                nc.vector.tensor_tensor(prob[:, j, 0:2], prob[:, j, 0:2], prob[:, j, 2:4], ALU.add).then_inc(s_add[s][j], 1)
                dve.wait_ge(s_add[s][j], cur)
                wait(dve, s_sT[o][j], left)
                nc.vector.scalar_tensor_tensor(out=dense[:, j], in0=prob[:, j, 0], scalar=1.0, in1=prob[:, j, 1],
                                               op0=ALU.mult, op1=ALU.add,
                                               accum_out=mass[:, s, j:j + 1]).then_inc(s_dense[s][j], 1)
                dve.wait_ge(s_dense[s][j], cur)
                nc.vector.tensor_scalar(dense[:, j, NE - 1:NE], dense[:, j, NE - 1:NE], mass[:, s, j:j + 1], float(H),
                                        ALU.subtract, ALU.add).then_inc(s_fix[s][j], 1)

            def weigh(s, cur, prev, o, left, j):
                dve.wait_ge(s_sT[s][j], cur)
                dve.wait_ge(s_mlp[s][3], cur)
                wait(dve, s_y[o][j], left)
                nc.vector.tensor_tensor(wT[:, j], bank[ST][:, :].rearrange("p (c t) -> p c t", c=FC),
                                        sproj[:, s, :, j * P:(j + 1) * P], ALU.mult).then_inc(s_wT[s][j], 1)

            def residual(s, cur, j):
                dve.wait_ge(s_y[s][j], cur)
                src, dst = (xin, x1) if s == 0 else (x2, x3)
                nc.vector.scalar_tensor_tensor(out=dst[:, j], in0=bank[Y][:, 0:D], scalar=0.5, in1=src[:, j],
                                               op0=ALU.mult, op1=ALU.add).then_inc(s_res[s][j], 1)

            def step(n2, n1, n0, first, second):
                ps = passes(n1, n0, first, second)
                if second:
                    normalise(LN2, n0, n0)
                for s, cur, prev, o, left in ps:
                    search(s, cur)
                for s, cur, prev, o, left in ps:
                    softmax_sum(s, cur)
                for s, cur, prev, o, left in ps:
                    softmax_bias(s, cur)
                p0 = ps[0]
                s, cur = p0[0], p0[1]
                if s == 1:
                    for j in range(NJ):
                        if j == 0:
                            dve.wait_ge(s_out, 16 * n0)
                        choose(*p0, j)
                        weigh(*p0, j)
                        residual(s, cur, j)
                    return
                choose(*p0, 0)
                weigh(*p0, 0)
                wait(dve, s_x2, n0)
                choose(*p0, 1)
                residual(s, cur, 0)
                weigh(*p0, 1)
                dve.wait_ge(s_res[0][0], n1)
                statistics(LNA, n1, 0)
                residual(s, cur, 1)
                dve.wait_ge(s_res[0][1], n1)
                statistics(LNA, n1, 1)
                variance(LNA, n1, n0)
                if second:
                    choose(*ps[1], 0)
                normalise(LNA, n1, n0)
                if second:
                    weigh(*ps[1], 0)
                dve.wait_ge(s_scp, n1)
                nc.vector.tensor_tensor(sc[:, :], bank[AUX][:, 0:3 * P], causal[:, :], ALU.add).then_inc(s_sc, 1)
                dve.wait_ge(s_sc, n1)
                nc.vector.reduce_max(mx[:, 0:1], sc[:, 0:P], AX.X)
                nc.vector.reduce_max(mx[:, 1:2], sc[:, P:3 * P], AX.X).then_inc(s_mx, 1)
                dve.wait_ge(s_mx, n1)
                nc.vector.tensor_scalar(nmx[:, :], mx[:, :], -SCALE, None, ALU.mult).then_inc(s_nmx, 1)
                if second:
                    dve.wait_ge(s_out, n0 * 16)
                    residual(1, n1, 0)
                dve.wait_ge(s_x, n2 * 16)
                for j in range(NJ):
                    statistics(LN1, n2, j)
                variance(LN1, n2, n1)
                if second:
                    choose(*ps[1], 1)
                normalise(LN1, n2, n1)
                dve.wait_ge(s_pr, n1)
                nc.vector.reciprocal(rinv[:, :], rs[:, :]).then_inc(s_rinv, 1)
                if second:
                    weigh(*ps[1], 1)
                    residual(1, n1, 1)
                    dve.wait_ge(s_res[1][1], n1)
                dve.wait_ge(s_rinv, n1)
                dve.wait_ge(s_o, n1)
                for j in range(NJ):
                    ins = nc.vector.scalar_tensor_tensor(out=x2[:, j], in0=bank[AUX][:, j * P:(j + 1) * P],
                                                         scalar=rinv[:, j:j + 1], in1=x1[:, j],
                                                         op0=ALU.mult, op1=ALU.add)
                ins.then_inc(s_x2, 1)
                dve.wait_ge(s_x2, n1)
                for j in range(NJ):
                    statistics(LN2, n1, j)
                variance(LN2, n1, n0)

            skip_pass_1(dve, s_hn[LN2], s_best[1], s_cand[1], s_top[1], s_dtop[1], s_z[1], s_nb[1], s_mask[1], s_add[1],
                        s_dense[1], s_fix[1], s_wT[1], s_res[1])
            steps(dve, step)

        @block.tensor
        def _(pe):
            mm, tr = nc.tensor.matmul, nc.tensor.transpose

            def transpose_h(ln, count):
                pe.wait_ge(s_hn[ln], count)
                for j in range(NJ):
                    ins = tr(bank[AUX][:, j * P:(j + 1) * P], hn[:, ln, j], ident[:, :])
                ins.then_inc(s_hTp[ln], 1)

            pe.wait_ge(s_const, 5)
            transpose_h(LN1, 1)
            pe.wait_ge(s_ld["wq"], 16)
            for g in range(2 * H):
                ins = tr(bank[g // H][0:NQ, (g % H) * D:(g % H + 1) * D], wq[:, g * NQ:(g + 1) * NQ], ident[:, :])
                if g % H == H - 1 and g < H:
                    ins.then_inc(s_tr[0], 1)
            pe.wait_ge(s_ld["keys"], 16)
            for side in range(2):
                for h in range(H):
                    g = side * H + h
                    ins = tr(bank[2][0:NQ, g * NK:(g + 1) * NK], keys[:, h, side * NQ:(side + 1) * NQ],
                             ident[0:NK, 0:NK])
            ins.then_inc(s_tr[1], 1)
            pe.wait_ge(s_ld["down"], 16)
            for c in range(FC):
                ins = tr(bank[3][:, c * P:(c + 1) * P], down[:, c], ident[:, :])
            ins.then_inc(s_tr[2], 1)
            pe.wait_ge(s_trc[0], 3)
            for g in range(2 * H):
                ins = mm(bank[4][:, g * NK:(g + 1) * NK], wqT[:, g], keyT[:, g], start=True, stop=True)
            ins.then_inc(s_fold[0], 1)
            pe.wait_ge(s_ld["qk"], 32)
            tr(bank[5][:, 0:D], qw[:, :], ident[:, :])
            tr(bank[5][:, D:2 * D], kw[:, :], ident[:, :])
            pe.wait_ge(s_ld["b"], 32)
            tr(bank[5][:, 2 * D:2 * D + 2 * FC], brow[:, :], ident[0:2 * FC, 0:2 * FC]).then_inc(s_tr[3], 1)
            pe.wait_ge(s_trc[2], 2)
            mm(bank[6][:, 0:D], qwT[:, :], kwT[:, :], start=True, stop=True).then_inc(s_fold[1], 1)
            pe.wait_ge(s_foldc[0], 1)
            pe.wait_ge(s_trc[1], 1)
            pe.wait_ge(s_foldc[1], 1)
            for name in ("wg", "wu", "vw", "wd", "up", "bd"):
                pe.wait_ge(s_ld[name], 16)

            def hidden(s, cur, prev, o, left):
                ln = LN1 if s == 0 else LN2
                pe.wait_ge(s_hT[ln], cur)
                for j in range(NJ):
                    wait(pe, s_sim[o][j], left)
                    mm(bank[SIM + j][:, :], hT[:, ln, j * P:(j + 1) * P], router[:, :], start=True,
                       stop=True).then_inc(s_simp[s][j], 1)
                for k in range(6):
                    if k < 3:
                        wait(pe, s_mlp[o][k + 3], left)
                    else:
                        pe.wait_ge(s_mlp[s][k - 3], cur)
                    w = (wg, downT, wu)[k // 2]
                    for i in range(2):
                        c = 2 * (k % 2) + i
                        ins = mm(bank[MLP + k % 3][:, i * S:(i + 1) * S], w[:, c * P:(c + 1) * P], hT[:, ln], start=True,
                                 stop=True)
                    ins.then_inc(s_mlpp[s][k], 1)

            def turn(s, cur, prev, o, left, j):
                pe.wait_ge(s_fix[s][j], cur)
                if j == 0:
                    wait(pe, s_wT[o][NJ - 1], left)
                else:
                    pe.wait_ge(s_wT[s][j - 1], cur)
                for c in range(FC):
                    ins = tr(bank[ST][:, c * P:(c + 1) * P], dense[:, j, c * P:(c + 1) * P], ident[:, :])
                ins.then_inc(s_sT[s][j], 1)

            def output(s, cur, prev, o, left, j):
                if j == 0:
                    wait(pe, s_res[o][NJ - 1], left)
                else:
                    pe.wait_ge(s_res[s][j - 1], cur)
                pe.wait_ge(s_act[s], cur)
                y = bank[Y][:, 0:D]
                mm(y, ones[:, :], bd[:, :], start=True, stop=False)
                for c in range(FC):
                    mm(y, act[:, s, c, j * P:(j + 1) * P], wd[:, c], start=False, stop=False)
                pe.wait_ge(s_wT[s][j], cur)
                for c in range(FC):
                    ins = mm(y, wT[:, j, c], up[:, c], start=False, stop=c == FC - 1)
                ins.then_inc(s_y[s][j], 1)

            def step(n2, n1, n0, first, second):
                ps = passes(n1, n0, first, second)
                for p_ in ps:
                    if p_[0] == 1:
                        transpose_h(LN2, n1)
                    hidden(*p_)
                p0 = ps[0]
                for j in range(NJ):
                    turn(*p0, j)
                    output(*p0, j)
                if not first:
                    return
                transpose_h(LNA, n1)
                pe.wait_ge(s_hT[LNA], n1)
                mm(bank[AUX][:, 0:S], qk[:, :], hT[:, LNA], start=True, stop=True)
                for j in range(NJ):
                    ins = mm(bank[AUX][:, S + j * P:S + (j + 1) * P], hT[:, LNA, j * P:(j + 1) * P], vw[:, :],
                             start=True, stop=True)
                ins.then_inc(s_tvp, 1)
                pe.wait_ge(s_tv, n1)
                mm(bank[AUX][:, 0:P], tv[:, 0:P], hT[:, LNA, 0:P], start=True, stop=True)
                mm(bank[AUX][:, P:3 * P], tv[:, P:2 * P], hT[:, LNA], start=True, stop=True).then_inc(s_scp, 1)
                if second:
                    turn(*ps[1], 0)
                    output(*ps[1], 0)
                pe.wait_ge(s_sc, n1)
                transpose_h(LN1, n2)
                if second:
                    turn(*ps[1], 1)
                    output(*ps[1], 1)
                pe.wait_ge(s_hT[LN1], n2)
                pe.wait_ge(s_pr, n1)
                for b in range(3):
                    ins = tr(bank[AUX][:, b * P:(b + 1) * P], pr[:, b * P:(b + 1) * P], ident[:, :])
                ins.then_inc(s_prTp, 1)
                pe.wait_ge(s_prT, n1)
                o = bank[AUX]
                mm(o[:, 0:D], prT[:, 0:P], tv[:, S:S + D], start=True, stop=True)
                mm(o[:, D:2 * D], prT[:, P:2 * P], tv[:, S:S + D], start=True, stop=False)
                mm(o[:, D:2 * D], prT[:, 2 * P:3 * P], tv[:, S + D:S + 2 * D], start=False, stop=True).then_inc(s_o, 1)

            skip_pass_1(pe, s_hTp[LN2], s_simp[1], s_mlpp[1], s_sT[1], s_y[1])
            steps(pe, step)


_INS = ["L0_attn_x", "L0_attn_Qw", "L0_attn_Kw", "L0_attn_Vw", "L0_ffn_Wg", "L0_ffn_bg", "L0_ffn_Wu", "L0_ffn_bu",
        "L0_ffn_Wd", "L0_ffn_bd", "L0_ffn_Wq", "L0_ffn_keys", "L0_ffn_down_embed", "L0_ffn_up_embed"]


def kernel(**inputs):
    import concourse.bacc as bacc
    from concourse.bass_utils import run_bass_kernel_spmd

    nc = bacc.Bacc("TRN2", target_bir_lowering=False, num_devices=1)
    arrays, args = {}, []
    for name in _INS:
        a = np.ascontiguousarray(inputs[name])
        arrays["in_" + name] = a
        args.append(nc.dram_tensor("in_" + name, a.shape, mybir.dt.from_np(a.dtype), kind="ExternalInput").ap())
    args.append(nc.dram_tensor("out_x", (B, S, D), mybir.dt.float32, kind="ExternalOutput").ap())
    build(nc, *args)
    r = run_bass_kernel_spmd(nc, [arrays], core_ids=[0])
    return r.results[0]["out_x"]
```

```python
import numpy as np
import concourse.bass as bass
from concourse import mybir
from contextlib import ExitStack

B, S, D = 8, 256, 128
P = 128
NJ = S // P
F = 512
NE = 512
H, NK, NQ, TOP = 4, 64, 64, 8
NX = NE // NK
FC = F // P
G = NJ * H
NC = 24
EPS = 1e-5
SCALE = float(D) ** -0.5
NEG = -1e30


def build(nc, x_d, qw_d, kw_d, vw_d, wg_d, bg_d, wu_d, bu_d, wd_d, bd_d, wq_d, keys_d, down_d, up_d, out_d):
    f32 = mybir.dt.float32
    ALU = mybir.AluOpType
    ACT = mybir.ActivationFunctionType
    AX = mybir.AxisListType

    ctx = ExitStack()
    with ctx:
        def sb(name, shape):
            return ctx.enter_context(nc.sbuf_tensor(name, shape, f32))

        def sem(name):
            return ctx.enter_context(nc.semaphore(name))

        def sems(name, *dims):
            if not dims:
                return sem(name)
            return [sems(f"{name}_{k}", *dims[1:]) for k in range(dims[0])]

        wg = sb("wg", [P, F]); wu = sb("wu", [P, F]); wq = sb("wq", [P, 2 * H * NQ])
        wd = sb("wd", [P, FC, D]); up = sb("up", [P, FC, D]); down = sb("down", [P, FC, D])
        keys = sb("keys", [NK, H, 2 * NQ])
        qw = sb("qw", [P, D]); kw = sb("kw", [P, D]); vw = sb("vw", [P, D])
        brow = sb("brow", [2 * FC, P]); bias = sb("bias", [P, 2 * FC]); bd = sb("bd", [1, D])
        ident = sb("ident", [P, P])
        ones = sb("ones", [1, P])
        half = sb("half", [P, 2 * NJ])
        causal = sb("causal", [P, 3 * P])
        wqT = sb("wqT", [NQ, 2 * H, D])
        keyT = sb("keyT", [NQ, 2 * H, NK])
        qwT = sb("qwT", [P, D]); kwT = sb("kwT", [P, D])
        router = sb("router", [P, 2 * H * NK])
        qk = sb("qk", [P, D])
        downT = sb("downT", [P, NE])
        xin = sb("xin", [P, NJ, D])
        xres = sb("xres", [P, NJ, D])
        x1 = sb("x1", [P, NJ, D])
        x2 = sb("x2", [P, NJ, D])
        x3 = sb("x3", [P, NJ, D])
        LN2, LN1, LNA = 0, 1, 2
        stats = sb("stats", [P, 3, NJ, 6])
        mv = sb("mv", [P, 3, NJ, 2])
        vare = sb("vare", [P, 3, NJ])
        rstd = sb("rstd", [P, 3, NJ])
        hn = sb("hn", [P, 3, NJ, D])
        hT = sb("hT", [P, 3, S])
        sims = sb("sims", [P, 2, NJ, 2, H * NK])
        best = sb("best", [P, 2, 2, G, TOP])
        cand = sb("cand", [P, 2, G, NC])
        top = sb("top", [P, 2, G, TOP])
        dtop = sb("dtop", [P, 2, G, TOP])
        etop = sb("etop", [P, 2, G, TOP])
        zsum = sb("zsum", [P, 2, G])
        lnz = sb("lnz", [P, 2, G])
        nbias = sb("nbias", [P, 2, G])
        gate = sb("gate", [P, 2, FC, S])
        upv = sb("upv", [P, 2, FC, S])
        act = sb("act", [P, 2, FC, S])
        sproj = sb("sproj", [P, 2, FC, S])
        pair = sb("pair", [P, 2, NJ, H, NX * NK])
        prob = sb("prob", [P, 2, NJ, H, NX * NK])
        dense = sb("dense", [P, NJ, NE])
        mass = sb("mass", [P, 2, NJ])
        wT = sb("wT", [P, NJ, FC, P])
        tv = sb("tv", [P, 2 * S])
        sc = sb("sc", [P, 3 * P])
        mx = sb("mx", [P, NJ]); nmx = sb("nmx", [P, NJ])
        pr = sb("pr", [P, 3 * P]); rs = sb("rs", [P, NJ]); rinv = sb("rinv", [P, NJ])
        prT = sb("prT", [P, 3 * P])

        bank = [ctx.enter_context(nc.psum_tensor(f"bank{i}", [P, 512], f32)) for i in range(8)]
        SIM, MLP, ST, Y, AUX = 0, 2, 5, 6, 7

        s_ld = {n: sem("ld_" + n) for n in ("wg", "wu", "wq", "wd", "up", "down", "keys", "qk", "vw", "b", "bd")}
        s_zero = sem("zeroed"); s_const = sem("constants")
        s_tr = sems("weights_transposed", 4)
        s_trc = sems("weights_transposed_copied", 4)
        s_fold = sems("weights_folded", 2)
        s_foldc = sems("weights_folded_copied", 2)
        s_x = sem("xin_loaded"); s_xr = sem("xres_loaded"); s_out = sem("x3_stored"); s_keep = sem("x2_kept")
        LNP = 0
        s_stat = sems("ln_stats", 2); s_mv = sems("ln_mean_var", 2); s_vare = sems("ln_var_eps", 2)
        s_rstd = sems("ln_rstd", 2); s_hn = sems("ln_normalised", 2); s_hTp = sems("ln_transposed", 2)
        s_hT = sems("ln_transposed_copied", 2)
        s_simp = sems("sims_multiplied", 2, NJ); s_sim = sems("sims_copied", 2, NJ)
        s_best = sems("side_best", 2); s_cand = sems("candidates", 2); s_top = sems("pair_best", 2)
        s_dtop = sems("top_shifted", 2); s_etop = sems("top_exp", 2); s_z = sems("softmax_sum", 2)
        s_lnz = sems("softmax_ln", 2); s_nb = sems("softmax_bias", 2)
        s_fill = sems("product_ready", 12); s_drain = sems("product_copied", 12)
        s_act = sems("act_ready", 2)
        s_pair = sems("pair_sums", 2, NJ); s_exp = sems("pair_exp", 2, NJ); s_mask = sems("pair_masked", 2, NJ)
        s_add = sems("heads_added_once", 2, NJ); s_dense = sems("heads_added", 2, NJ); s_fix = sems("last_row", 2, NJ)
        s_sT = sems("dense_transposed", 2, NJ); s_wT = sems("weights_ready", 2, NJ)
        s_y = sems("ffn_multiplied", 2, NJ); s_res = sems("ffn_added", 2, NJ)
        s_tvp = sem("att_tv_multiplied"); s_tv = sem("att_tv_copied"); s_scp = sem("att_scores")
        s_sc = sem("att_masked"); s_mx = sem("att_max"); s_nmx = sem("att_bias"); s_pr = sem("att_probs")
        s_prTp = sem("att_probs_transposed"); s_prT = sem("att_probs_copied"); s_o = sem("att_out")
        s_rinv = sem("att_rinv"); s_x2 = sem("att_added")

        block = ctx.enter_context(nc.Block())

        def wait(eng, s, v):
            if not (isinstance(v, int) and v <= 0):
                eng.wait_ge(s, v)

        FULL = dict(now=True, late=True, ahead=True, far=True)
        FIRST = dict(now=False, late=False, ahead=True, far=True)
        SECOND = dict(now=True, late=False, ahead=True, far=True)
        LAST_BUT_ONE = dict(now=True, late=True, ahead=False, far=False)
        LAST = dict(now=False, late=True, ahead=False, far=False)
        NONE = dict(now=False, late=False, ahead=False, far=False)

        def steps(eng, step):
            step([-1, 0, 1, 2], FIRST, NONE)
            step([0, 1, 2, 3], SECOND, FIRST)
            with eng.Fori(1, B - 1) as it:
                n = [it]
                for k in (1, 2, 3):
                    reg = eng.alloc_register(f"step_plus_{k}")
                    eng.reg_add(reg, it, k)
                    n.append(eng.snap(reg, donate=True))
                step(n, FULL, FULL)
            step([B - 1, B, B + 1, B + 2], LAST_BUT_ONE, FULL)
            step([B, B + 1, B + 2, B + 3], LAST, LAST_BUT_ONE)

        def head_counts(n, s):
            return (n[1], n[2]) if s == 0 else (n[0], n[1])

        def left_by(n, runs, s):
            return (0, n[1]) if s == 1 and runs["now"] else (1, n[0])

        def skip_pass_1(eng, *lists):
            for s in lists:
                for x in s if isinstance(s, list) else [s]:
                    eng.sem_inc(x, 1)

        EXPERTS, GATE, UP = range(3)
        FILLS = ([(0, EXPERTS, c, "now") for c in (0, 2)]
                 + [(1, w, c, "late") for w in (GATE, EXPERTS, UP) for c in (0, 2)]
                 + [(0, w, c, "ahead") for w in (GATE, UP) for c in (0, 2)])

        def fill_count(n, q, before=False):
            return n[(2 if FILLS[q][3] == "ahead" else 1) - before]

        def bank_left(n, q, runs, ran):
            for p in range(q - 3, -1, -3):
                if runs[FILLS[p][3]]:
                    return p, fill_count(n, p)
            for p in range(9 + q % 3, -1, -3):
                if ran[FILLS[p][3]]:
                    return p, fill_count(n, p, before=True)
            return None

        def fills_of(s, *kinds):
            return [q for q, f in enumerate(FILLS) if f[0] == s and f[1] in kinds]

        @block.sync
        def _(sp):
            for name, dst, src in (("wq", wq[:, :], wq_d), ("down", down[:, :, :], down_d.rearrange("(c p) d -> p c d", p=P)),
                                   ("wg", wg[:, :], wg_d), ("wu", wu[:, :], wu_d),
                                   ("up", up[:, :, :], up_d.rearrange("(c p) d -> p c d", p=P))):
                sp.dma_start(dst, src).then_inc(s_ld[name], 16)
            sp.dma_start(bd[:, :], bd_d.rearrange("(o d) -> o d", o=1)).then_inc(s_ld["bd"], 16)

            def load(b, count):
                sp.wait_ge(s_hn[LNP], count)
                sp.dma_start(xin[:, :, :], x_d[b].rearrange("(j p) d -> p j d", p=P)).then_inc(s_x, 16)

            def load_residual(b, count):
                for j in range(NJ):
                    wait(sp, s_res[0][j], count)
                sp.dma_start(xres[:, :, :], x_d[b].rearrange("(j p) d -> p j d", p=P)).then_inc(s_xr, 16)

            def store(b, count):
                for j in range(NJ):
                    sp.wait_ge(s_res[1][j], count)
                sp.dma_start(out_d[b].rearrange("(j p) d -> p j d", p=P), x3[:, :, :]).then_inc(s_out, 16)

            sp.sem_inc(s_out, 16)
            load(1, 1)
            load_residual(0, 0)
            load(2, 2)
            load_residual(1, 1)
            with sp.Fori(1, B - 2) as it:
                load(it + 2, it + 2)
                load_residual(it + 1, it + 1)
                store(it - 1, it + 1)
            load(B - 1, B)
            load_residual(B - 1, B - 1)
            store(B - 3, B - 1)
            store(B - 2, B)
            store(B - 1, B + 1)
            sp.wait_ge(s_out, 16 * (B + 1))

        @block.gpsimd
        def _(pool):
            nc.gpsimd.memset(ident[:, :], 0.0).then_inc(s_zero, 1)
            nc.gpsimd.memset(causal[:, :], 0.0).then_inc(s_zero, 1)
            pool.wait_ge(s_zero, 2)
            nc.gpsimd.affine_select(out=ident[:, :], in_=ident[:, :], compare_op=ALU.not_equal, fill=1.0, base=0,
                                    pattern=[[-1, P]], channel_multiplier=1).then_inc(s_const, 1)
            for b in (0, 2):
                blk = causal[:, b * P:(b + 1) * P]
                nc.gpsimd.affine_select(out=blk, in_=blk, compare_op=ALU.is_ge, fill=NEG, base=0,
                                        pattern=[[-1, P]], channel_multiplier=1).then_inc(s_const, 1)
            nc.gpsimd.memset(half[:, :], -0.5).then_inc(s_const, 1)
            nc.gpsimd.memset(ones[:, :], 1.0).then_inc(s_const, 1)
            pool.wait_ge(s_const, 5)

            def power(group, lo, hi, count):
                pool.wait_ge(s_vare[group], count)
                nc.gpsimd.tensor_tensor(rstd[:, lo:hi].rearrange("p l j -> p (l j)"),
                                        vare[:, lo:hi].rearrange("p l j -> p (l j)"),
                                        half[:, 0:NJ * (hi - lo)], ALU.pow).then_inc(s_rstd[group], 1)

            def product(n, s):
                before, after = head_counts(n, s)
                wait(pool, s_y[s][NJ - 1], before)
                for q in fills_of(s, GATE, UP):
                    pool.wait_ge(s_drain[q], after)
                nc.gpsimd.tensor_tensor(act[:, s], gate[:, s], upv[:, s], ALU.mult).then_inc(s_act[s], 1)

            def sums(n, s, j):
                before, after = head_counts(n, s)
                pool.wait_ge(s_sim[s][j], after)
                wait(pool, s_mask[s][j], before)
                simx = sims[:, s, j, 0].rearrange("p (h k) -> p h k", h=H)[:, :, 0:NX]
                simy = sims[:, s, j, 1].rearrange("p (h k) -> p h k", h=H)
                nc.gpsimd.tensor_tensor(pair[:, s, j].rearrange("p h (x y) -> p h x y", x=NX),
                                        simx.unsqueeze(3).to_broadcast([P, H, NX, NK]),
                                        simy.unsqueeze(2).to_broadcast([P, H, NX, NK]), ALU.add).then_inc(s_pair[s][j], 1)

            def step(n, runs, ran):
                if runs["late"]:
                    sums(n, 1, 0)
                    sums(n, 1, 1)
                    product(n, 1)
                if runs["ahead"]:
                    sums(n, 0, 0)
                if runs["now"]:
                    power(1, LNA, LNA + 1, n[1])
                if runs["ahead"]:
                    sums(n, 0, 1)
                    product(n, 0)
                if runs["now"] or runs["far"]:
                    power(LNP, LN2 if runs["now"] else LN1, LN1 + 1 if runs["far"] else LN1, n[3])

            power(LNP, LN1, LN1 + 1, 1)
            skip_pass_1(pool, s_pair[1], s_act[1])
            steps(pool, step)

        @block.scalar
        def _(act_):
            act_.dma_start(xin[:, :, :], x_d[0].rearrange("(j p) d -> p j d", p=P)).then_inc(s_x, 16)
            act_.dma_start(keys[:, :, :], keys_d.rearrange("h k s n -> k h (s n)")).then_inc(s_ld["keys"], 16)
            act_.dma_start(qw[:, :], qw_d).then_inc(s_ld["qk"], 16)
            act_.dma_start(kw[:, :], kw_d).then_inc(s_ld["qk"], 16)
            act_.dma_start(brow[0:FC, :], bg_d.rearrange("(c p) -> c p", p=P)).then_inc(s_ld["b"], 16)
            act_.dma_start(brow[FC:2 * FC, :], bu_d.rearrange("(c p) -> c p", p=P)).then_inc(s_ld["b"], 16)
            act_.dma_start(vw[:, :], vw_d).then_inc(s_ld["vw"], 16)
            act_.dma_start(wd[:, :, :], wd_d.rearrange("(c p) d -> p c d", p=P)).then_inc(s_ld["wd"], 16)

            def copy_hT(group, lo, hi, count):
                act_.wait_ge(s_hTp[group], count)
                at = (lo % 2) * S if group == LNP else 0
                nc.scalar.copy(hT[:, lo:hi].rearrange("p l t -> p (l t)"),
                               bank[AUX][:, at:at + (hi - lo) * S]).then_inc(s_hT[group], 1)

            act_.wait_ge(s_tr[0], 1)
            nc.scalar.copy(wqT[:, 0:H].rearrange("p g d -> p (g d)"), bank[0][0:NQ, :]).then_inc(s_trc[0], 1)
            act_.wait_ge(s_tr[1], 1)
            nc.scalar.copy(wqT[:, H:2 * H].rearrange("p g d -> p (g d)"), bank[1][0:NQ, :]).then_inc(s_trc[0], 1)
            nc.scalar.copy(keyT[:, :, :].rearrange("p g k -> p (g k)"), bank[2][0:NQ, :]).then_inc(s_trc[0], 1)
            act_.wait_ge(s_tr[2], 1)
            nc.scalar.copy(downT[:, :], bank[3][:, :]).then_inc(s_trc[1], 1)
            act_.wait_ge(s_fold[0], 1)
            nc.scalar.copy(router[:, :], bank[4][:, :]).then_inc(s_foldc[0], 1)
            act_.wait_ge(s_tr[3], 1)
            nc.scalar.copy(qwT[:, :], bank[5][:, 0:D]).then_inc(s_trc[2], 1)
            nc.scalar.copy(kwT[:, :], bank[5][:, D:2 * D]).then_inc(s_trc[2], 1)
            nc.scalar.copy(bias[:, :], bank[5][:, 2 * D:2 * D + 2 * FC]).then_inc(s_trc[3], 1)
            act_.wait_ge(s_trc[3], 1)
            act_.wait_ge(s_fold[1], 1)
            nc.scalar.copy(qk[:, :], bank[6][:, 0:D]).then_inc(s_foldc[1], 1)

            def copy_sims(n, s):
                before, after = head_counts(n, s)
                for j in range(NJ):
                    act_.wait_ge(s_simp[s][j], after)
                    wait(act_, s_pair[s][j], before)
                    wait(act_, s_best[s], before)
                    nc.scalar.copy(sims[:, s, j].rearrange("p a k -> p (a k)"), bank[SIM + j][:, :]).then_inc(s_sim[s][j], 1)

            def drain(n, q):
                s, kind, c, part = FILLS[q]
                act_.wait_ge(s_fill[q], fill_count(n, q))
                if kind == EXPERTS:
                    for j in range(NJ):
                        wait(act_, s_wT[s][j], n[0])
                    ins = nc.scalar.activation(sproj[:, s, c:c + 2].rearrange("p c t -> p (c t)"),
                                               bank[MLP + q % 3][:, :], ACT.Silu)
                else:
                    wait(act_, s_act[s], fill_count(n, q, before=True))
                    dst, func, b0 = (gate, ACT.Silu, 0) if kind == GATE else (upv, ACT.Identity, FC)
                    for i in range(2):
                        ins = nc.scalar.activation(dst[:, s, c + i], bank[MLP + q % 3][:, i * S:(i + 1) * S], func,
                                                   bias=bias[:, b0 + c + i:b0 + c + i + 1])
                ins.then_inc(s_drain[q], 1)

            def top_exp(n, s):
                act_.wait_ge(s_dtop[s], head_counts(n, s)[1])
                nc.scalar.activation(etop[:, s], dtop[:, s], ACT.Exp).then_inc(s_etop[s], 1)

            def sum_ln(n, s):
                act_.wait_ge(s_z[s], head_counts(n, s)[1])
                nc.scalar.activation(lnz[:, s], zsum[:, s], ACT.Ln).then_inc(s_lnz[s], 1)

            def exps(n, s, j):
                before, after = head_counts(n, s)
                act_.wait_ge(s_nb[s], after)
                act_.wait_ge(s_pair[s][j], after)
                wait(act_, s_dense[s][j], before)
                for h in range(H):
                    ins = nc.scalar.activation(prob[:, s, j, h], pair[:, s, j, h], ACT.Exp,
                                               bias=nbias[:, s, j * H + h:j * H + h + 1])
                ins.then_inc(s_exp[s][j], 1)

            def keep(n):
                act_.wait_ge(s_out, n[0] * 16)
                act_.wait_ge(s_x2, n[0])
                nc.scalar.copy(x3[:, :, :].rearrange("p j d -> p (j d)"),
                               x2[:, :, :].rearrange("p j d -> p (j d)")).then_inc(s_keep, 1)

            def step(n, runs, ran):
                if runs["now"]:
                    for q in fills_of(0, EXPERTS):
                        drain(n, q)
                if runs["late"] or runs["ahead"]:
                    copy_hT(LNP, LN2 if runs["late"] else LN1, LN1 + 1 if runs["ahead"] else LN1, n[2])
                if runs["late"]:
                    copy_sims(n, 1)
                    for q in fills_of(1, GATE, EXPERTS, UP):
                        drain(n, q)
                    keep(n)
                if runs["ahead"]:
                    copy_sims(n, 0)
                    for q in fills_of(0, GATE, UP):
                        drain(n, q)
                nc.scalar.preload_act_table_set("natural_log_exp_and_others")
                if runs["late"]:
                    top_exp(n, 1)
                    sum_ln(n, 1)
                    exps(n, 1, 0)
                if runs["now"]:
                    copy_hT(1, LNA, LNA + 1, n[1])
                    act_.wait_ge(s_tvp, n[1])
                    nc.scalar.copy(tv[:, :], bank[AUX][:, :]).then_inc(s_tv, 1)
                if runs["ahead"]:
                    top_exp(n, 0)
                if runs["late"]:
                    exps(n, 1, 1)
                if runs["ahead"]:
                    sum_ln(n, 0)
                if runs["now"]:
                    act_.wait_ge(s_nmx, n[1])
                    act_.wait_ge(s_sc, n[1])
                    nc.scalar.activation(pr[:, 0:P], sc[:, 0:P], ACT.Exp, bias=nmx[:, 0:1], scale=SCALE,
                                         accum_out=rs[:, 0:1])
                    nc.scalar.activation(pr[:, P:3 * P], sc[:, P:3 * P], ACT.Exp, bias=nmx[:, 1:2], scale=SCALE,
                                         accum_out=rs[:, 1:2]).then_inc(s_pr, 1)
                    act_.wait_ge(s_prTp, n[1])
                    nc.scalar.copy(prT[:, :], bank[AUX][:, 0:3 * P]).then_inc(s_prT, 1)
                if runs["ahead"]:
                    exps(n, 0, 0)
                    exps(n, 0, 1)

            skip_pass_1(act_, s_keep, s_sim[1], [s_drain[q] for q in fills_of(1, GATE, EXPERTS, UP)], s_etop[1], s_lnz[1],
                        s_exp[1])
            steps(act_, step)

        @block.vector
        def _(dve):
            src_of = {LN1: xin, LNA: x1, LN2: x2}

            def static_wait():
                dve.wait_ge(s_const, 5)

            def statistics(ln, j):
                return nc.vector.bn_stats(stats[:, ln, j], src_of[ln][:, j])

            def variance(group, lo, hi, before, after):
                static_wait()
                dve.wait_ge(s_stat[group], after)
                for ln in range(lo, hi):
                    for j in range(NJ):
                        ins = nc.vector.bn_aggr(mv[:, ln, j], stats[:, ln, j])
                ins.then_inc(s_mv[group], 1)
                dve.wait_ge(s_mv[group], after)
                wait(dve, s_rstd[group], before)
                nc.vector.tensor_scalar_add(vare[:, lo:hi], mv[:, lo:hi, :, 1], EPS).then_inc(s_vare[group], 1)

            def normalise(group, lo, hi, before, after):
                dve.wait_ge(s_rstd[group], after)
                wait(dve, s_hTp[group], before)
                for ln in range(lo, hi):
                    for j in range(NJ):
                        ins = nc.vector.tensor_scalar(hn[:, ln, j], src_of[ln][:, j], mv[:, ln, j, 0:1],
                                                      rstd[:, ln, j:j + 1], ALU.subtract, ALU.mult)
                ins.then_inc(s_hn[group], 1)

            dve.wait_ge(s_x, 16)
            for j in range(NJ):
                ins = statistics(LN1, j)
            ins.then_inc(s_stat[LNP], 1)
            variance(LNP, LN1, LN1 + 1, 0, 1)
            normalise(LNP, LN1, LN1 + 1, 0, 1)

            def search(n, s):
                cur = head_counts(n, s)[1]
                for j in range(NJ):
                    static_wait()
                    dve.wait_ge(s_sim[s][j], cur)
                    for side in range(2):
                        for h in range(H):
                            ins = nc.vector.max(best[:, s, side, j * H + h], sims[:, s, j, side, h * NK:(h + 1) * NK])
                ins.then_inc(s_best[s], 1)
                dve.wait_ge(s_best[s], cur)
                bx, by = best[:, s, 0], best[:, s, 1]
                nc.vector.tensor_tensor(cand[:, s, :, 0:8], bx[:, :, 0:1].to_broadcast([P, G, 8]), by, ALU.add)
                nc.vector.tensor_tensor(cand[:, s, :, 8:20].rearrange("p g (a b) -> p g a b", a=3),
                                        bx[:, :, 1:4].unsqueeze(3).to_broadcast([P, G, 3, 4]),
                                        by[:, :, 0:4].unsqueeze(2).to_broadcast([P, G, 3, 4]), ALU.add)
                nc.vector.tensor_tensor(cand[:, s, :, 20:24], bx[:, :, 4:8], by[:, :, 0:1].to_broadcast([P, G, 4]),
                                        ALU.add).then_inc(s_cand[s], 1)
                static_wait()
                dve.wait_ge(s_cand[s], cur)
                for g in range(G):
                    ins = nc.vector.max(top[:, s, g], cand[:, s, g])
                ins.then_inc(s_top[s], 1)
                dve.wait_ge(s_top[s], cur)
                nc.vector.tensor_tensor(dtop[:, s], top[:, s], top[:, s, :, 0:1].to_broadcast([P, G, TOP]),
                                        ALU.subtract).then_inc(s_dtop[s], 1)

            def softmax_sum(n, s):
                cur = head_counts(n, s)[1]
                dve.wait_ge(s_etop[s], cur)
                nc.vector.tensor_reduce(zsum[:, s], etop[:, s], AX.X, ALU.add).then_inc(s_z[s], 1)

            def softmax_bias(n, s):
                cur = head_counts(n, s)[1]
                dve.wait_ge(s_lnz[s], cur)
                nc.vector.scalar_tensor_tensor(out=nbias[:, s], in0=top[:, s, :, 0], scalar=-1.0, in1=lnz[:, s],
                                               op0=ALU.mult, op1=ALU.subtract).then_inc(s_nb[s], 1)

            def mask(n, s, j):
                dve.wait_ge(s_exp[s][j], n[1])
                for h in range(H):
                    ins = nc.vector.scalar_tensor_tensor(out=prob[:, s, j, h], in0=pair[:, s, j, h],
                                                         scalar=top[:, s, j * H + h, TOP - 1:TOP], in1=prob[:, s, j, h],
                                                         op0=ALU.is_ge, op1=ALU.mult)
                ins.then_inc(s_mask[s][j], 1)

            def add_heads(n, runs, s, j):
                dve.wait_ge(s_mask[s][j], n[1])
                nc.vector.tensor_tensor(prob[:, s, j, 0:2], prob[:, s, j, 0:2], prob[:, s, j, 2:4],
                                        ALU.add).then_inc(s_add[s][j], 1)
                dve.wait_ge(s_add[s][j], n[1])
                o, left = left_by(n, runs, s)
                wait(dve, s_sT[o][j], left)
                nc.vector.scalar_tensor_tensor(out=dense[:, j], in0=prob[:, s, j, 0], scalar=1.0, in1=prob[:, s, j, 1],
                                               op0=ALU.mult, op1=ALU.add,
                                               accum_out=mass[:, s, j:j + 1]).then_inc(s_dense[s][j], 1)
                dve.wait_ge(s_dense[s][j], n[1])
                nc.vector.tensor_scalar(dense[:, j, NE - 1:NE], dense[:, j, NE - 1:NE], mass[:, s, j:j + 1], float(H),
                                        ALU.subtract, ALU.add).then_inc(s_fix[s][j], 1)

            def weigh(n, runs, s, j):
                dve.wait_ge(s_sT[s][j], n[1])
                dve.wait_ge(s_drain[fills_of(s, EXPERTS)[-1]], n[1])
                o, left = left_by(n, runs, s)
                wait(dve, s_y[o][j], left)
                nc.vector.tensor_tensor(wT[:, j], bank[ST][:, :].rearrange("p (c t) -> p c t", c=FC),
                                        sproj[:, s, :, j * P:(j + 1) * P], ALU.mult).then_inc(s_wT[s][j], 1)

            def residual(n, s, j):
                dve.wait_ge(s_y[s][j], n[1])
                if s == 0:
                    dve.wait_ge(s_xr, n[1] * 16)
                else:
                    dve.wait_ge(s_keep, n[1])
                src, dst = (xres, x1) if s == 0 else (x3, x3)
                nc.vector.scalar_tensor_tensor(out=dst[:, j], in0=bank[Y][:, 0:D], scalar=0.5, in1=src[:, j],
                                               op0=ALU.mult, op1=ALU.add).then_inc(s_res[s][j], 1)

            def scores(n):
                dve.wait_ge(s_scp, n[1])
                nc.vector.tensor_tensor(sc[:, :], bank[AUX][:, 0:3 * P], causal[:, :], ALU.add).then_inc(s_sc, 1)
                dve.wait_ge(s_sc, n[1])
                nc.vector.reduce_max(mx[:, 0:1], sc[:, 0:P], AX.X)
                nc.vector.reduce_max(mx[:, 1:2], sc[:, P:3 * P], AX.X).then_inc(s_mx, 1)
                dve.wait_ge(s_mx, n[1])
                nc.vector.tensor_scalar(nmx[:, :], mx[:, :], -SCALE, None, ALU.mult).then_inc(s_nmx, 1)

            def attended(n, runs):
                dve.wait_ge(s_pr, n[1])
                nc.vector.reciprocal(rinv[:, :], rs[:, :]).then_inc(s_rinv, 1)
                if runs["late"]:
                    dve.wait_ge(s_keep, n[1])
                dve.wait_ge(s_rinv, n[1])
                dve.wait_ge(s_o, n[1])
                for j in range(NJ):
                    ins = nc.vector.scalar_tensor_tensor(out=x2[:, j], in0=bank[AUX][:, j * P:(j + 1) * P],
                                                         scalar=rinv[:, j:j + 1], in1=x1[:, j],
                                                         op0=ALU.mult, op1=ALU.add)
                ins.then_inc(s_x2, 1)

            def next_norms(n, runs):
                lo, hi = LN2 if runs["now"] else LN1, LN1 + 1 if runs["far"] else LN1
                if runs["far"]:
                    dve.wait_ge(s_x, n[3] * 16)
                    for j in range(NJ):
                        ins = statistics(LN1, j)
                if runs["now"]:
                    dve.wait_ge(s_x2, n[1])
                    for j in range(NJ):
                        ins = statistics(LN2, j)
                ins.then_inc(s_stat[LNP], 1)
                variance(LNP, lo, hi, n[2], n[3])

            def normalise_next(n, runs):
                normalise(LNP, LN2 if runs["now"] else LN1, LN1 + 1 if runs["far"] else LN1, n[2], n[3])

            def step(n, runs, ran):
                now, late, ahead = runs["now"], runs["late"], runs["ahead"]
                if now:
                    mask(n, 0, 0)
                    add_heads(n, runs, 0, 0)
                if late:
                    search(n, 1)
                if now:
                    weigh(n, runs, 0, 0)
                    mask(n, 0, 1)
                if late:
                    softmax_sum(n, 1)
                if now:
                    add_heads(n, runs, 0, 1)
                if late:
                    softmax_bias(n, 1)
                if now:
                    residual(n, 0, 0)
                if ahead:
                    search(n, 0)
                if now:
                    weigh(n, runs, 0, 1)
                    residual(n, 0, 1)
                    for j in range(NJ):
                        dve.wait_ge(s_res[0][j], n[1])
                        ins = statistics(LNA, j)
                    ins.then_inc(s_stat[1], 1)
                    variance(1, LNA, LNA + 1, n[0], n[1])
                if late:
                    mask(n, 1, 0)
                if now:
                    normalise(1, LNA, LNA + 1, n[0], n[1])
                if late:
                    add_heads(n, runs, 1, 0)
                if ahead:
                    softmax_sum(n, 0)
                if now:
                    scores(n)
                if ahead:
                    softmax_bias(n, 0)
                if late:
                    weigh(n, runs, 1, 0)
                    mask(n, 1, 1)
                if now:
                    attended(n, runs)
                if now or runs["far"]:
                    next_norms(n, runs)
                if late:
                    residual(n, 1, 0)
                    add_heads(n, runs, 1, 1)
                if now or runs["far"]:
                    normalise_next(n, runs)
                if late:
                    weigh(n, runs, 1, 1)
                    residual(n, 1, 1)

            skip_pass_1(dve, s_best[1], s_cand[1], s_top[1], s_dtop[1], s_z[1], s_nb[1], s_mask[1], s_add[1],
                        s_dense[1], s_fix[1], s_wT[1], s_res[1])
            steps(dve, step)

        @block.tensor
        def _(pe):
            mm, tr = nc.tensor.matmul, nc.tensor.transpose

            def transpose_h(group, lo, hi, count):
                pe.wait_ge(s_hn[group], count)
                for ln in range(lo, hi):
                    for j in range(NJ):
                        at = ((ln % 2) * S if group == LNP else 0) + j * P
                        ins = tr(bank[AUX][:, at:at + P], hn[:, ln, j], ident[:, :])
                ins.then_inc(s_hTp[group], 1)

            pe.wait_ge(s_const, 5)
            pe.wait_ge(s_ld["wq"], 16)
            for g in range(2 * H):
                ins = tr(bank[g // H][0:NQ, (g % H) * D:(g % H + 1) * D], wq[:, g * NQ:(g + 1) * NQ], ident[:, :])
                if g % H == H - 1 and g < H:
                    ins.then_inc(s_tr[0], 1)
            pe.wait_ge(s_ld["keys"], 16)
            for side in range(2):
                for h in range(H):
                    g = side * H + h
                    ins = tr(bank[2][0:NQ, g * NK:(g + 1) * NK], keys[:, h, side * NQ:(side + 1) * NQ],
                             ident[0:NK, 0:NK])
            ins.then_inc(s_tr[1], 1)
            pe.wait_ge(s_ld["down"], 16)
            for c in range(FC):
                ins = tr(bank[3][:, c * P:(c + 1) * P], down[:, c], ident[:, :])
            ins.then_inc(s_tr[2], 1)
            pe.wait_ge(s_trc[0], 3)
            for g in range(2 * H):
                ins = mm(bank[4][:, g * NK:(g + 1) * NK], wqT[:, g], keyT[:, g], start=True, stop=True)
            ins.then_inc(s_fold[0], 1)
            pe.wait_ge(s_ld["qk"], 32)
            tr(bank[5][:, 0:D], qw[:, :], ident[:, :])
            tr(bank[5][:, D:2 * D], kw[:, :], ident[:, :])
            pe.wait_ge(s_ld["b"], 32)
            tr(bank[5][:, 2 * D:2 * D + 2 * FC], brow[:, :], ident[0:2 * FC, 0:2 * FC]).then_inc(s_tr[3], 1)
            pe.wait_ge(s_trc[2], 2)
            mm(bank[6][:, 0:D], qwT[:, :], kwT[:, :], start=True, stop=True).then_inc(s_fold[1], 1)
            pe.wait_ge(s_foldc[0], 1)
            pe.wait_ge(s_trc[1], 1)
            pe.wait_ge(s_foldc[1], 1)
            for name in ("wg", "wu", "vw", "wd", "up", "bd"):
                pe.wait_ge(s_ld[name], 16)

            def similarities(n, s, ran):
                before, after = head_counts(n, s)
                ln = LN2 if s == 1 else LN1
                for j in range(NJ):
                    wait(pe, s_sim[1 - s][j], n[1] if s == 0 or ran["ahead"] else n[0])
                    wait(pe, s_sim[s][j], before)
                    mm(bank[SIM + j][:, :], hT[:, ln, j * P:(j + 1) * P], router[:, :], start=True,
                       stop=True).then_inc(s_simp[s][j], 1)

            def fill(n, q, runs, ran):
                s, kind, c, part = FILLS[q]
                last = bank_left(n, q, runs, ran)
                if last:
                    wait(pe, s_drain[last[0]], last[1])
                w = {EXPERTS: downT, GATE: wg, UP: wu}[kind]
                for i in range(2):
                    ins = mm(bank[MLP + q % 3][:, i * S:(i + 1) * S], w[:, (c + i) * P:(c + i + 1) * P],
                             hT[:, LN2 if s == 1 else LN1], start=True, stop=True)
                ins.then_inc(s_fill[q], 1)

            def turn(n, runs, s, j):
                pe.wait_ge(s_fix[s][j], n[1])
                if j == 0:
                    o, left = left_by(n, runs, s)
                    wait(pe, s_wT[o][NJ - 1], left)
                else:
                    pe.wait_ge(s_wT[s][j - 1], n[1])
                for c in range(FC):
                    ins = tr(bank[ST][:, c * P:(c + 1) * P], dense[:, j, c * P:(c + 1) * P], ident[:, :])
                ins.then_inc(s_sT[s][j], 1)

            def output(n, runs, s, j):
                if j == 0:
                    o, left = left_by(n, runs, s)
                    wait(pe, s_res[o][NJ - 1], left)
                else:
                    pe.wait_ge(s_res[s][j - 1], n[1])
                pe.wait_ge(s_act[s], n[1])
                y = bank[Y][:, 0:D]
                mm(y, ones[:, :], bd[:, :], start=True, stop=False)
                for c in range(FC):
                    mm(y, act[:, s, c, j * P:(j + 1) * P], wd[:, c], start=False, stop=False)
                pe.wait_ge(s_wT[s][j], n[1])
                for c in range(FC):
                    ins = mm(y, wT[:, j, c], up[:, c], start=False, stop=c == FC - 1)
                ins.then_inc(s_y[s][j], 1)

            def attention_in(n):
                transpose_h(1, LNA, LNA + 1, n[1])
                pe.wait_ge(s_hT[1], n[1])
                mm(bank[AUX][:, 0:S], qk[:, :], hT[:, LNA], start=True, stop=True)
                for j in range(NJ):
                    ins = mm(bank[AUX][:, S + j * P:S + (j + 1) * P], hT[:, LNA, j * P:(j + 1) * P], vw[:, :],
                             start=True, stop=True)
                ins.then_inc(s_tvp, 1)
                pe.wait_ge(s_tv, n[1])
                mm(bank[AUX][:, 0:P], tv[:, 0:P], hT[:, LNA, 0:P], start=True, stop=True)
                mm(bank[AUX][:, P:3 * P], tv[:, P:2 * P], hT[:, LNA], start=True, stop=True).then_inc(s_scp, 1)

            def attention_out(n):
                pe.wait_ge(s_sc, n[1])
                pe.wait_ge(s_pr, n[1])
                for b in range(3):
                    ins = tr(bank[AUX][:, b * P:(b + 1) * P], pr[:, b * P:(b + 1) * P], ident[:, :])
                ins.then_inc(s_prTp, 1)
                pe.wait_ge(s_prT, n[1])
                o = bank[AUX]
                mm(o[:, 0:D], prT[:, 0:P], tv[:, S:S + D], start=True, stop=True)
                mm(o[:, D:2 * D], prT[:, P:2 * P], tv[:, S:S + D], start=True, stop=False)
                mm(o[:, D:2 * D], prT[:, 2 * P:3 * P], tv[:, S + D:S + 2 * D], start=False, stop=True).then_inc(s_o, 1)

            def step(n, runs, ran):
                now, late, ahead = runs["now"], runs["late"], runs["ahead"]
                if now:
                    for q in fills_of(0, EXPERTS):
                        fill(n, q, runs, ran)
                if late or ahead:
                    transpose_h(LNP, LN2 if late else LN1, LN1 + 1 if ahead else LN1, n[2])
                    pe.wait_ge(s_hT[LNP], n[2])
                if late:
                    similarities(n, 1, ran)
                    for q in fills_of(1, GATE):
                        fill(n, q, runs, ran)
                if now:
                    turn(n, runs, 0, 0)
                if late:
                    for q in fills_of(1, EXPERTS):
                        fill(n, q, runs, ran)
                if ahead:
                    similarities(n, 0, ran)
                if now:
                    output(n, runs, 0, 0)
                if late:
                    for q in fills_of(1, UP):
                        fill(n, q, runs, ran)
                if ahead:
                    for q in fills_of(0, GATE, UP):
                        fill(n, q, runs, ran)
                if now:
                    turn(n, runs, 0, 1)
                    output(n, runs, 0, 1)
                    attention_in(n)
                if late:
                    turn(n, runs, 1, 0)
                    output(n, runs, 1, 0)
                if now:
                    attention_out(n)
                if late:
                    turn(n, runs, 1, 1)
                    output(n, runs, 1, 1)

            skip_pass_1(pe, s_simp[1], [s_fill[q] for q in fills_of(1, GATE, EXPERTS, UP)], s_sT[1], s_y[1])
            steps(pe, step)


_INS = ["L0_attn_x", "L0_attn_Qw", "L0_attn_Kw", "L0_attn_Vw", "L0_ffn_Wg", "L0_ffn_bg", "L0_ffn_Wu", "L0_ffn_bu",
        "L0_ffn_Wd", "L0_ffn_bd", "L0_ffn_Wq", "L0_ffn_keys", "L0_ffn_down_embed", "L0_ffn_up_embed"]


def kernel(**inputs):
    import concourse.bacc as bacc
    from concourse.bass_utils import run_bass_kernel_spmd

    nc = bacc.Bacc("TRN2", target_bir_lowering=False, num_devices=1)
    arrays, args = {}, []
    for name in _INS:
        a = np.ascontiguousarray(inputs[name])
        arrays["in_" + name] = a
        args.append(nc.dram_tensor("in_" + name, a.shape, mybir.dt.from_np(a.dtype), kind="ExternalInput").ap())
    args.append(nc.dram_tensor("out_x", (B, S, D), mybir.dt.float32, kind="ExternalOutput").ap())
    build(nc, *args)
    r = run_bass_kernel_spmd(nc, [arrays], core_ids=[0])
    return r.results[0]["out_x"]
```

```python
import numpy as np
import concourse.bass as bass
from concourse import mybir
from contextlib import ExitStack

B, S, D = 8, 256, 128
P = 128
NJ = S // P
F = 512
NE = 512
H, NK, NQ, TOP = 4, 64, 64, 8
NX = NE // NK
FC = F // P
G = NJ * H
NC = 24
EPS = 1e-5
SCALE = float(D) ** -0.5
NEG = -1e30


def build(nc, x_d, qw_d, kw_d, vw_d, wg_d, bg_d, wu_d, bu_d, wd_d, bd_d, wq_d, keys_d, down_d, up_d, out_d):
    f32 = mybir.dt.float32
    ALU = mybir.AluOpType
    ACT = mybir.ActivationFunctionType
    AX = mybir.AxisListType

    ctx = ExitStack()
    with ctx:
        def sb(name, shape):
            return ctx.enter_context(nc.sbuf_tensor(name, shape, f32))

        def sem(name):
            return ctx.enter_context(nc.semaphore(name))

        def sems(name, *dims):
            if not dims:
                return sem(name)
            return [sems(f"{name}_{k}", *dims[1:]) for k in range(dims[0])]

        wg = sb("wg", [P, F]); wu = sb("wu", [P, F]); wq = sb("wq", [P, 2 * H * NQ])
        wd = sb("wd", [P, FC, D]); up = sb("up", [P, FC, D]); down = sb("down", [P, FC, D])
        keys = sb("keys", [NK, H, 2 * NQ])
        qw = sb("qw", [P, D]); kw = sb("kw", [P, D]); vw = sb("vw", [P, D])
        brow = sb("brow", [2 * FC, P]); bias = sb("bias", [P, 2 * FC]); bd = sb("bd", [1, D])
        ident = sb("ident", [P, P])
        ones = sb("ones", [1, P])
        half = sb("half", [P, NJ])
        causal = sb("causal", [P, 3 * P])
        wqT = sb("wqT", [NQ, 2 * H, D])
        keyT = sb("keyT", [NQ, 2 * H, NK])
        qwT = sb("qwT", [P, D]); kwT = sb("kwT", [P, D])
        router = sb("router", [P, 2 * H * NK])
        qk = sb("qk", [P, D])
        downT = sb("downT", [P, NE])
        xin = sb("xin", [P, NJ, D])
        xres = sb("xres", [P, NJ, D])
        x1 = sb("x1", [P, NJ, D])
        x2 = sb("x2", [P, NJ, D])
        x3 = sb("x3", [P, NJ, D])
        LN1, LN2, LNA = 0, 1, 2
        stats = sb("stats", [P, 3, NJ, 6])
        mv = sb("mv", [P, 3, NJ, 2])
        vare = sb("vare", [P, 3, NJ])
        rstd = sb("rstd", [P, 3, NJ])
        hn = sb("hn", [P, 3, NJ, D])
        hT = sb("hT", [P, 3, S])
        sims = sb("sims", [P, 2, NJ, 2, H * NK])
        best = sb("best", [P, 2, 2, G, TOP])
        cand = sb("cand", [P, 2, G, NC])
        top = sb("top", [P, 2, G, TOP])
        dtop = sb("dtop", [P, 2, G, TOP])
        etop = sb("etop", [P, 2, G, TOP])
        zsum = sb("zsum", [P, 2, G])
        lnz = sb("lnz", [P, 2, G])
        nbias = sb("nbias", [P, 2, G])
        gate = sb("gate", [P, 2, FC, S])
        upv = sb("upv", [P, 2, FC, S])
        act = sb("act", [P, 2, FC, S])
        sproj = sb("sproj", [P, 2, FC, S])
        pair = sb("pair", [P, 2, NJ, H, NX * NK])
        prob = sb("prob", [P, 2, NJ, H, NX * NK])
        dense = sb("dense", [P, NJ, NE])
        mass = sb("mass", [P, 2, NJ])
        wT = sb("wT", [P, NJ, FC, P])
        tv = sb("tv", [P, 2 * S])
        sc = sb("sc", [P, 3 * P])
        mx = sb("mx", [P, NJ]); nmx = sb("nmx", [P, NJ])
        pr = sb("pr", [P, 3 * P]); rs = sb("rs", [P, NJ]); rinv = sb("rinv", [P, NJ])
        prT = sb("prT", [P, 3 * P])

        bank = [ctx.enter_context(nc.psum_tensor(f"bank{i}", [P, 512], f32)) for i in range(8)]
        SIM, MLP, ST, Y, AUX = 0, 2, 5, 6, 7

        s_ld = {n: sem("loaded_" + n) for n in ("wq", "down", "keys", "qk", "b", "mlp", "others")}
        s_zero = sem("zeroed"); s_const = sem("constants")
        s_tr = sems("weights_transposed", 4)
        s_trc = sems("weights_transposed_copied", 4)
        s_fold = sems("weights_folded", 2)
        s_foldc = sems("weights_folded_copied", 2)
        s_x = sem("xin_loaded"); s_xr = sem("xres_loaded"); s_out = sem("x3_stored"); s_keep = sem("x2_kept")
        s_stat = sems("ln_stats", 3); s_mv = sems("ln_mean_var", 3); s_vare = sems("ln_var_eps", 3)
        s_rstd = sems("ln_rstd", 3); s_hn = sems("ln_normalised", 3); s_hTp = sems("ln_transposed", 3)
        s_hT = sems("ln_transposed_copied", 3)
        s_simp = sems("sims_multiplied", 2, NJ); s_sim = sems("sims_copied", 2, NJ)
        s_best = sems("side_best", 2, NJ); s_cand = sems("candidates", 2); s_top = sems("pair_best", 2)
        s_dtop = sems("top_shifted", 2); s_etop = sems("top_exp", 2); s_z = sems("softmax_sum", 2)
        s_lnz = sems("softmax_ln", 2); s_nb = sems("softmax_bias", 2)
        s_fill = sems("product_ready", 2, 3, FC // 2); s_drain = sems("product_copied", 2, 3, FC // 2)
        s_act = sems("act_ready", 2)
        s_pair = sems("pair_sums", 2, NJ); s_exp = sems("pair_exp", 2, NJ); s_mask = sems("pair_masked", 2, NJ)
        s_add = sems("heads_added_once", 2, NJ); s_dense = sems("heads_added", 2, NJ); s_fix = sems("last_row", 2, NJ)
        s_sT = sems("dense_transposed", 2, NJ); s_wT = sems("weights_ready", 2, NJ)
        s_ym = sems("mlp_multiplied", 2, NJ); s_y = sems("ffn_multiplied", 2, NJ); s_res = sems("ffn_added", 2, NJ)
        s_tvp = sem("att_tv_multiplied"); s_tv = sem("att_tv_copied"); s_scp = sem("att_scores")
        s_sc = sem("att_masked"); s_mx = sem("att_max"); s_nmx = sem("att_bias"); s_pr = sem("att_probs")
        s_prTp = sem("att_probs_transposed"); s_prT = sem("att_probs_copied"); s_o = sem("att_out")
        s_rinv = sem("att_rinv"); s_x2 = sem("att_added")

        block = ctx.enter_context(nc.Block())

        def wait(eng, s, v):
            if not (isinstance(v, int) and v <= 0):
                eng.wait_ge(s, v)

        class Step:
            def __init__(self, it, counts=None):
                self.it, self.counts = it, counts

            def count(self, k):
                return self.counts[k] if self.counts else self.it + k

            def runs(self, k):
                return bool(self.counts) or 0 <= self.it + k < B

        class Batch:
            def __init__(self, step, k):
                self.step, self.k = step, k
                self.number = self.before = step.count(k)
                self.after = step.count(k + 1)

        def is_first(b):
            return isinstance(b.number, int) and b.number == 0

        def do(step, k, stage, *args):
            if step.runs(k):
                stage(Batch(step, k), *args)

        def steps(eng, run, ahead):
            for it in range(-ahead, 1):
                run(Step(it))
            with eng.Fori(1, B - ahead) as it:
                counts = [it]
                for k in range(1, ahead + 2):
                    reg = eng.alloc_register(f"step_plus_{k}")
                    eng.reg_add(reg, it, k)
                    counts.append(eng.snap(reg, donate=True))
                run(Step(None, counts))
            for it in range(B - ahead, B):
                run(Step(it))

        def user_before(order, step, me):
            for back in range(1, len(order) * B):
                i, k = (me - back) % len(order), order[(me - back) % len(order)][-1]
                rounds = -((me - back) // len(order))
                if step.runs(k - rounds):
                    return i, step.count(k - rounds + 1)
            return None

        src_of = {LN1: xin, LNA: x1, LN2: x2}

        EXPERTS, GATE, UP = range(3)
        SIM_ORDER = [[(1, 1), (0, 3)], [(1, 1), (0, 3)]]
        MLP_ORDER = [[(0, EXPERTS, 0, 2), (1, GATE, 0, 1), (0, GATE, 2, 3), (0, UP, 0, 3)],
                     [(1, EXPERTS, 0, 1), (1, UP, 2, 1), (0, UP, 2, 3), (0, EXPERTS, 2, 3)],
                     [(1, GATE, 2, 1), (0, GATE, 0, 3), (1, UP, 0, 1), (1, EXPERTS, 2, 1)]]
        ST_ORDER = [(1, 0, 0), (1, 1, 0), (0, 0, 2), (0, 1, 2)]
        Y_ORDER = [(1, 1, 0), (0, 0, 2), (0, 1, 2), (1, 0, 1)]
        AUX_ORDER = [(s_x2, 1), (s_hT[LN2], 1), (s_hT[LN1], 3), (s_hT[LNA], 2), (s_tv, 2), (s_sc, 2), (s_prT, 2)]
        DENSE_ORDER = [[(0, 2), (1, 1)], [(0, 2), (1, 1)]]
        WT_ORDER = [[(0, 2), (1, 1)], [(1, 0), (0, 2)]]
        FUSED = (1,)

        def mlp_bank(s, kind, c):
            return next(MLP + i for i, order in enumerate(MLP_ORDER) for user in order if user[:-1] == (s, kind, c))

        def place(order, *me):
            return next(i for i, user in enumerate(order) if user[:-1] == me)

        @block.sync
        def _(sp):
            for name, dst, src in (("wq", wq[:, :], wq_d),
                                   ("down", down[:, :, :], down_d.rearrange("(c p) d -> p c d", p=P)),
                                   ("qk", qw[:, :], qw_d), ("qk", kw[:, :], kw_d),
                                   ("b", brow[0:FC, :], bg_d.rearrange("(c p) -> c p", p=P)),
                                   ("b", brow[FC:2 * FC, :], bu_d.rearrange("(c p) -> c p", p=P)),
                                   ("mlp", wg[:, :], wg_d), ("mlp", wu[:, :], wu_d),
                                   ("others", vw[:, :], vw_d),
                                   ("others", wd[:, :, :], wd_d.rearrange("(c p) d -> p c d", p=P)),
                                   ("others", up[:, :, :], up_d.rearrange("(c p) d -> p c d", p=P)),
                                   ("others", bd[:, :], bd_d.rearrange("(o d) -> o d", o=1))):
                sp.dma_start(dst, src).then_inc(s_ld[name], 16)

            def load(b):
                if is_first(b):
                    return
                sp.wait_ge(s_hn[LN1], b.before)
                sp.dma_start(xin[:, :, :], x_d[b.number].rearrange("(j p) d -> p j d", p=P)).then_inc(s_x, 16)

            def load_residual(b):
                for j in range(NJ):
                    wait(sp, s_res[0][j], b.before)
                sp.dma_start(xres[:, :, :], x_d[b.number].rearrange("(j p) d -> p j d", p=P)).then_inc(s_xr, 16)

            def store(b):
                for j in range(NJ):
                    sp.wait_ge(s_res[1][j], b.after)
                sp.dma_start(out_d[b.number].rearrange("(j p) d -> p j d", p=P), x3[:, :, :]).then_inc(s_out, 16)

            def run(step):
                do(step, 1, load_residual)
                do(step, 3, load)
                do(step, 0, store)

            steps(sp, run, 3)
            sp.wait_ge(s_out, 16 * B)

        @block.gpsimd
        def _(pool):
            nc.gpsimd.memset(ident[:, :], 0.0).then_inc(s_zero, 1)
            nc.gpsimd.memset(causal[:, :], 0.0).then_inc(s_zero, 1)
            pool.wait_ge(s_zero, 2)
            nc.gpsimd.affine_select(out=ident[:, :], in_=ident[:, :], compare_op=ALU.not_equal, fill=1.0, base=0,
                                    pattern=[[-1, P]], channel_multiplier=1).then_inc(s_const, 1)
            for b in (0, 2):
                blk = causal[:, b * P:(b + 1) * P]
                nc.gpsimd.affine_select(out=blk, in_=blk, compare_op=ALU.is_ge, fill=NEG, base=0,
                                        pattern=[[-1, P]], channel_multiplier=1).then_inc(s_const, 1)
            nc.gpsimd.memset(half[:, :], -0.5).then_inc(s_const, 1)
            nc.gpsimd.memset(ones[:, :], 1.0).then_inc(s_const, 1)
            pool.wait_ge(s_const, 5)

            def power(b, ln):
                pool.wait_ge(s_vare[ln], b.after)
                nc.gpsimd.tensor_tensor(rstd[:, ln], vare[:, ln], half[:, :], ALU.pow).then_inc(s_rstd[ln], 1)

            def product(b, s):
                for j in range(NJ):
                    wait(pool, s_ym[s][j], b.before)
                for kind in (GATE, UP):
                    for c in range(FC // 2):
                        pool.wait_ge(s_drain[s][kind][c], b.after)
                nc.gpsimd.tensor_tensor(act[:, s], gate[:, s], upv[:, s], ALU.mult).then_inc(s_act[s], 1)

            def pair_sums(b, s, j):
                pool.wait_ge(s_sim[s][j], b.after)
                wait(pool, s_mask[s][j], b.before)
                simx = sims[:, s, j, 0].rearrange("p (h k) -> p h k", h=H)[:, :, 0:NX]
                simy = sims[:, s, j, 1].rearrange("p (h k) -> p h k", h=H)
                nc.gpsimd.tensor_tensor(pair[:, s, j].rearrange("p h (x y) -> p h x y", x=NX),
                                        simx.unsqueeze(3).to_broadcast([P, H, NX, NK]),
                                        simy.unsqueeze(2).to_broadcast([P, H, NX, NK]),
                                        ALU.add).then_inc(s_pair[s][j], 1)

            def candidates(b, s):
                for j in range(NJ):
                    pool.wait_ge(s_best[s][j], b.after)
                wait(pool, s_top[s], b.before)
                bx, by = best[:, s, 0], best[:, s, 1]
                nc.gpsimd.tensor_tensor(cand[:, s, :, 0:8], bx[:, :, 0:1].to_broadcast([P, G, 8]), by, ALU.add)
                nc.gpsimd.tensor_tensor(cand[:, s, :, 8:20].rearrange("p g (a b) -> p g a b", a=3),
                                        bx[:, :, 1:4].unsqueeze(3).to_broadcast([P, G, 3, 4]),
                                        by[:, :, 0:4].unsqueeze(2).to_broadcast([P, G, 3, 4]), ALU.add)
                nc.gpsimd.tensor_tensor(cand[:, s, :, 20:24], bx[:, :, 4:8], by[:, :, 0:1].to_broadcast([P, G, 4]),
                                        ALU.add).then_inc(s_cand[s], 1)

            def add_heads(b, s, j):
                pool.wait_ge(s_mask[s][j], b.after)
                nc.gpsimd.tensor_tensor(prob[:, s, j, 0:2], prob[:, s, j, 0:2], prob[:, s, j, 2:4],
                                        ALU.add).then_inc(s_add[s][j], 1)

            def run(step):
                do(step, 2, pair_sums, 0, 1)
                do(step, 0, add_heads, 1, 0)
                do(step, 0, add_heads, 1, 1)
                do(step, 3, power, LN1)
                do(step, 1, power, LN2)
                do(step, 2, product, 0)
                do(step, 2, add_heads, 0, 0)
                do(step, 2, add_heads, 0, 1)
                do(step, 1, pair_sums, 1, 0)
                do(step, 3, pair_sums, 0, 0)
                do(step, 3, candidates, 0)
                do(step, 2, power, LNA)
                do(step, 1, pair_sums, 1, 1)

            steps(pool, run, 3)

        @block.scalar
        def _(act_):
            act_.dma_start(xin[:, :, :], x_d[0].rearrange("(j p) d -> p j d", p=P)).then_inc(s_x, 16)
            act_.dma_start(keys[:, :, :], keys_d.rearrange("h k s n -> k h (s n)")).then_inc(s_ld["keys"], 16)

            act_.wait_ge(s_tr[0], 1)
            nc.scalar.copy(wqT[:, 0:H].rearrange("p g d -> p (g d)"), bank[0][0:NQ, :]).then_inc(s_trc[0], 1)
            act_.wait_ge(s_tr[0], 2)
            nc.scalar.copy(wqT[:, H:2 * H].rearrange("p g d -> p (g d)"), bank[1][0:NQ, :]).then_inc(s_trc[0], 1)
            act_.wait_ge(s_tr[1], 1)
            nc.scalar.copy(keyT[:, :, :].rearrange("p g k -> p (g k)"), bank[2][0:NQ, :]).then_inc(s_trc[0], 1)
            act_.wait_ge(s_tr[2], 1)
            nc.scalar.copy(downT[:, :], bank[3][:, :]).then_inc(s_trc[1], 1)
            act_.wait_ge(s_fold[0], 1)
            nc.scalar.copy(router[:, :], bank[4][:, :]).then_inc(s_foldc[0], 1)
            act_.wait_ge(s_hTp[LN1], 1)
            nc.scalar.copy(hT[:, LN1], bank[AUX][:, 0:S]).then_inc(s_hT[LN1], 1)
            act_.wait_ge(s_tr[3], 1)
            nc.scalar.copy(qwT[:, :], bank[5][:, 0:D]).then_inc(s_trc[2], 1)
            nc.scalar.copy(kwT[:, :], bank[5][:, D:2 * D]).then_inc(s_trc[2], 1)
            nc.scalar.copy(bias[:, :], bank[5][:, 2 * D:2 * D + 2 * FC]).then_inc(s_trc[3], 1)

            def copy_hT(b, ln):
                if is_first(b) and ln == LN1:
                    return
                act_.wait_ge(s_hTp[ln], b.after)
                nc.scalar.copy(hT[:, ln], bank[AUX][:, 0:S]).then_inc(s_hT[ln], 1)

            def copy_sims(b, s, j):
                act_.wait_ge(s_simp[s][j], b.after)
                wait(act_, s_pair[s][j], b.before)
                wait(act_, s_best[s][j], b.before)
                nc.scalar.copy(sims[:, s, j].rearrange("p a k -> p (a k)"),
                               bank[SIM + j][:, :]).then_inc(s_sim[s][j], 1)
                if is_first(b) and (s, j) == (0, 1):
                    act_.wait_ge(s_fold[1], 1)
                    nc.scalar.copy(qk[:, :], bank[6][:, 0:D]).then_inc(s_foldc[1], 1)

            def drain(b, s, kind, c):
                act_.wait_ge(s_fill[s][kind][c // 2], b.after)
                src = bank[mlp_bank(s, kind, c)]
                if kind == EXPERTS:
                    for j in range(NJ):
                        wait(act_, s_wT[s][j], b.before)
                    ins = nc.scalar.activation(sproj[:, s, c:c + 2].rearrange("p c t -> p (c t)"), src[:, :], ACT.Silu)
                else:
                    if is_first(b):
                        act_.wait_ge(s_trc[3], 1)
                    wait(act_, s_drain[s][UP][c // 2] if s in FUSED else s_act[s], b.before)
                    dst, func, b0 = (gate, ACT.Silu, 0) if kind == GATE else (upv, ACT.Identity, FC)
                    for i in range(2):
                        ins = nc.scalar.activation(dst[:, s, c + i], src[:, i * S:(i + 1) * S], func,
                                                   bias=bias[:, b0 + c + i:b0 + c + i + 1])
                ins.then_inc(s_drain[s][kind][c // 2], 1)

            def exp_table(step):
                nc.scalar.preload_act_table_set("natural_log_exp_and_others")

            def top_exp(b, s):
                act_.wait_ge(s_dtop[s], b.after)
                nc.scalar.activation(etop[:, s], dtop[:, s], ACT.Exp).then_inc(s_etop[s], 1)

            def sum_ln(b, s):
                act_.wait_ge(s_z[s], b.after)
                nc.scalar.activation(lnz[:, s], zsum[:, s], ACT.Ln).then_inc(s_lnz[s], 1)

            def pair_exp(b, s, j):
                act_.wait_ge(s_nb[s], b.after)
                act_.wait_ge(s_pair[s][j], b.after)
                wait(act_, s_dense[s][j], b.before)
                for h in range(H):
                    ins = nc.scalar.activation(prob[:, s, j, h], pair[:, s, j, h], ACT.Exp,
                                               bias=nbias[:, s, j * H + h:j * H + h + 1])
                ins.then_inc(s_exp[s][j], 1)

            def copy_tv(b):
                act_.wait_ge(s_tvp, b.after)
                nc.scalar.copy(tv[:, :], bank[AUX][:, :]).then_inc(s_tv, 1)

            def score_exp(b):
                act_.wait_ge(s_nmx, b.after)
                act_.wait_ge(s_sc, b.after)
                nc.scalar.activation(pr[:, 0:P], sc[:, 0:P], ACT.Exp, bias=nmx[:, 0:1], scale=SCALE,
                                     accum_out=rs[:, 0:1])
                nc.scalar.activation(pr[:, P:3 * P], sc[:, P:3 * P], ACT.Exp, bias=nmx[:, 1:2], scale=SCALE,
                                     accum_out=rs[:, 1:2]).then_inc(s_pr, 1)

            def copy_probs(b):
                act_.wait_ge(s_prTp, b.after)
                nc.scalar.copy(prT[:, :], bank[AUX][:, 0:3 * P]).then_inc(s_prT, 1)

            def keep(b):
                if not (isinstance(b.before, int) and b.before <= 0):
                    act_.wait_ge(s_out, b.before * 16)
                act_.wait_ge(s_x2, b.after)
                nc.scalar.copy(x3[:, :, :].rearrange("p j d -> p (j d)"),
                               x2[:, :, :].rearrange("p j d -> p (j d)")).then_inc(s_keep, 1)

            def run(step):
                do(step, 0, drain, 1, EXPERTS, 0)
                do(step, 0, drain, 1, GATE, 2)
                do(step, 2, copy_sims, 0, 1)
                do(step, 0, drain, 1, GATE, 0)
                do(step, 2, drain, 0, GATE, 0)
                do(step, 2, drain, 0, GATE, 2)
                exp_table(step)
                do(step, 0, top_exp, 1)
                do(step, 0, sum_ln, 1)
                do(step, 0, pair_exp, 1, 0)
                do(step, 1, copy_hT, LNA)
                do(step, 2, drain, 0, UP, 2)
                do(step, 1, copy_tv)
                do(step, 2, top_exp, 0)
                do(step, 0, pair_exp, 1, 1)
                do(step, 1, score_exp)
                do(step, 0, keep)
                do(step, 2, drain, 0, UP, 0)
                do(step, 1, copy_probs)
                do(step, 2, sum_ln, 0)
                do(step, 0, drain, 1, EXPERTS, 2)
                exp_table(step)
                do(step, 2, pair_exp, 0, 0)
                do(step, 1, copy_hT, LN2)
                do(step, 2, pair_exp, 0, 1)
                do(step, 3, copy_hT, LN1)
                do(step, 1, copy_sims, 1, 0)
                do(step, 1, copy_sims, 1, 1)
                do(step, 2, drain, 0, EXPERTS, 2)
                do(step, 2, drain, 0, EXPERTS, 0)
                do(step, 3, copy_sims, 0, 0)

            steps(act_, run, 3)

        @block.vector
        def _(dve):
            def static_wait():
                dve.wait_ge(s_const, 5)

            def statistics(b, ln):
                if ln == LN1:
                    dve.wait_ge(s_x, b.after * 16)
                elif ln == LN2:
                    dve.wait_ge(s_x2, b.after)
                else:
                    for j in range(NJ):
                        dve.wait_ge(s_res[0][j], b.after)
                for j in range(NJ):
                    ins = nc.vector.bn_stats(stats[:, ln, j], src_of[ln][:, j])
                ins.then_inc(s_stat[ln], 1)

            def mean_variance(b, ln):
                static_wait()
                dve.wait_ge(s_stat[ln], b.after)
                for j in range(NJ):
                    ins = nc.vector.bn_aggr(mv[:, ln, j], stats[:, ln, j])
                ins.then_inc(s_mv[ln], 1)

            def add_eps(b, ln):
                dve.wait_ge(s_mv[ln], b.after)
                wait(dve, s_rstd[ln], b.before)
                nc.vector.tensor_scalar_add(vare[:, ln], mv[:, ln, :, 1], EPS).then_inc(s_vare[ln], 1)

            def normalise(b, ln):
                dve.wait_ge(s_rstd[ln], b.after)
                wait(dve, s_hTp[ln], b.before)
                for j in range(NJ):
                    ins = nc.vector.tensor_scalar(hn[:, ln, j], src_of[ln][:, j], mv[:, ln, j, 0:1],
                                                  rstd[:, ln, j:j + 1], ALU.subtract, ALU.mult)
                ins.then_inc(s_hn[ln], 1)

            def side_best(b, s, j):
                static_wait()
                dve.wait_ge(s_sim[s][j], b.after)
                wait(dve, s_cand[s], b.before)
                for side in range(2):
                    for h in range(H):
                        ins = nc.vector.max(best[:, s, side, j * H + h], sims[:, s, j, side, h * NK:(h + 1) * NK])
                ins.then_inc(s_best[s][j], 1)

            def candidates(b, s):
                for j in range(NJ):
                    dve.wait_ge(s_best[s][j], b.after)
                bx, by = best[:, s, 0], best[:, s, 1]
                nc.vector.tensor_tensor(cand[:, s, :, 0:8], bx[:, :, 0:1].to_broadcast([P, G, 8]), by, ALU.add)
                nc.vector.tensor_tensor(cand[:, s, :, 8:20].rearrange("p g (a b) -> p g a b", a=3),
                                        bx[:, :, 1:4].unsqueeze(3).to_broadcast([P, G, 3, 4]),
                                        by[:, :, 0:4].unsqueeze(2).to_broadcast([P, G, 3, 4]), ALU.add)
                nc.vector.tensor_tensor(cand[:, s, :, 20:24], bx[:, :, 4:8], by[:, :, 0:1].to_broadcast([P, G, 4]),
                                        ALU.add).then_inc(s_cand[s], 1)

            def pair_best(b, s):
                static_wait()
                dve.wait_ge(s_cand[s], b.after)
                wait(dve, s_dtop[s], b.before)
                for g in range(G):
                    ins = nc.vector.max(top[:, s, g], cand[:, s, g])
                ins.then_inc(s_top[s], 1)

            def shift_best(b, s):
                dve.wait_ge(s_top[s], b.after)
                nc.vector.tensor_tensor(dtop[:, s], top[:, s], top[:, s, :, 0:1].to_broadcast([P, G, TOP]),
                                        ALU.subtract).then_inc(s_dtop[s], 1)

            def softmax_sum(b, s):
                dve.wait_ge(s_etop[s], b.after)
                nc.vector.tensor_reduce(zsum[:, s], etop[:, s], AX.X, ALU.add).then_inc(s_z[s], 1)

            def softmax_bias(b, s):
                dve.wait_ge(s_lnz[s], b.after)
                nc.vector.scalar_tensor_tensor(out=nbias[:, s], in0=top[:, s, :, 0], scalar=-1.0, in1=lnz[:, s],
                                               op0=ALU.mult, op1=ALU.subtract).then_inc(s_nb[s], 1)

            def product(b, s):
                for j in range(NJ):
                    wait(dve, s_ym[s][j], b.before)
                for kind in (GATE, UP):
                    for c in range(FC // 2):
                        dve.wait_ge(s_drain[s][kind][c], b.after)
                nc.vector.tensor_tensor(act[:, s], gate[:, s], upv[:, s], ALU.mult).then_inc(s_act[s], 1)

            def gate_up(b, s, c):
                if is_first(b):
                    dve.wait_ge(s_trc[3], 1)
                dve.wait_ge(s_fill[s][UP][c // 2], b.after)
                dve.wait_ge(s_drain[s][GATE][c // 2], b.after)
                for j in range(NJ):
                    wait(dve, s_ym[s][j], b.before)
                for i in range(2):
                    ins = nc.vector.scalar_tensor_tensor(out=act[:, s, c + i],
                                                         in0=bank[mlp_bank(s, UP, c)][:, i * S:(i + 1) * S],
                                                         scalar=bias[:, FC + c + i:FC + c + i + 1],
                                                         in1=gate[:, s, c + i], op0=ALU.add, op1=ALU.mult)
                ins.then_inc(s_drain[s][UP][c // 2], 1)

            def mask(b, s, j):
                dve.wait_ge(s_exp[s][j], b.after)
                for h in range(H):
                    ins = nc.vector.scalar_tensor_tensor(out=prob[:, s, j, h], in0=pair[:, s, j, h],
                                                         scalar=top[:, s, j * H + h, TOP - 1:TOP], in1=prob[:, s, j, h],
                                                         op0=ALU.is_ge, op1=ALU.mult)
                ins.then_inc(s_mask[s][j], 1)

            def make_dense(b, s, j):
                dve.wait_ge(s_add[s][j], b.after)
                last = user_before(DENSE_ORDER[j], b.step, place(DENSE_ORDER[j], s))
                if last:
                    dve.wait_ge(s_sT[DENSE_ORDER[j][last[0]][0]][j], last[1])
                nc.vector.scalar_tensor_tensor(out=dense[:, j], in0=prob[:, s, j, 0], scalar=1.0, in1=prob[:, s, j, 1],
                                               op0=ALU.mult, op1=ALU.add,
                                               accum_out=mass[:, s, j:j + 1]).then_inc(s_dense[s][j], 1)

            def last_row(b, s, j):
                dve.wait_ge(s_dense[s][j], b.after)
                nc.vector.tensor_scalar(dense[:, j, NE - 1:NE], dense[:, j, NE - 1:NE], mass[:, s, j:j + 1], float(H),
                                        ALU.subtract, ALU.add).then_inc(s_fix[s][j], 1)

            def weigh(b, s, j):
                dve.wait_ge(s_sT[s][j], b.after)
                for c in range(FC // 2):
                    dve.wait_ge(s_drain[s][EXPERTS][c], b.after)
                last = user_before(WT_ORDER[j], b.step, place(WT_ORDER[j], s))
                if last:
                    dve.wait_ge(s_y[WT_ORDER[j][last[0]][0]][j], last[1])
                nc.vector.tensor_tensor(wT[:, j], bank[ST][:, :].rearrange("p (c t) -> p c t", c=FC),
                                        sproj[:, s, :, j * P:(j + 1) * P], ALU.mult).then_inc(s_wT[s][j], 1)

            def residual(b, s, j):
                dve.wait_ge(s_y[s][j], b.after)
                if s == 0:
                    dve.wait_ge(s_xr, b.after * 16)
                else:
                    dve.wait_ge(s_keep, b.after)
                src, dst = (xres, x1) if s == 0 else (x3, x3)
                nc.vector.scalar_tensor_tensor(out=dst[:, j], in0=bank[Y][:, 0:D], scalar=0.5, in1=src[:, j],
                                               op0=ALU.mult, op1=ALU.add).then_inc(s_res[s][j], 1)

            def mask_scores(b):
                dve.wait_ge(s_scp, b.after)
                nc.vector.tensor_tensor(sc[:, :], bank[AUX][:, 0:3 * P], causal[:, :], ALU.add).then_inc(s_sc, 1)

            def score_max(b):
                dve.wait_ge(s_sc, b.after)
                nc.vector.reduce_max(mx[:, 0:1], sc[:, 0:P], AX.X)
                nc.vector.reduce_max(mx[:, 1:2], sc[:, P:3 * P], AX.X).then_inc(s_mx, 1)

            def score_bias(b):
                dve.wait_ge(s_mx, b.after)
                nc.vector.tensor_scalar(nmx[:, :], mx[:, :], -SCALE, None, ALU.mult).then_inc(s_nmx, 1)

            def reciprocal(b):
                dve.wait_ge(s_pr, b.after)
                nc.vector.reciprocal(rinv[:, :], rs[:, :]).then_inc(s_rinv, 1)

            def add_attention(b):
                wait(dve, s_keep, b.before)
                dve.wait_ge(s_rinv, b.after)
                dve.wait_ge(s_o, b.after)
                for j in range(NJ):
                    ins = nc.vector.scalar_tensor_tensor(out=x2[:, j], in0=bank[AUX][:, j * P:(j + 1) * P],
                                                         scalar=rinv[:, j:j + 1], in1=x1[:, j],
                                                         op0=ALU.mult, op1=ALU.add)
                ins.then_inc(s_x2, 1)

            def run(step):
                do(step, 0, weigh, 1, 1)
                do(step, 2, mask, 0, 0)
                do(step, 0, residual, 1, 1)
                do(step, 2, mask, 0, 1)
                do(step, 2, make_dense, 0, 0)
                do(step, 1, side_best, 1, 0)
                do(step, 2, last_row, 0, 0)
                do(step, 1, side_best, 1, 1)
                do(step, 2, weigh, 0, 0)
                do(step, 1, candidates, 1)
                do(step, 2, make_dense, 0, 1)
                do(step, 1, pair_best, 1)
                do(step, 2, last_row, 0, 1)
                do(step, 1, shift_best, 1)
                do(step, 2, residual, 0, 0)
                do(step, 3, side_best, 0, 0)
                do(step, 2, weigh, 0, 1)
                do(step, 3, side_best, 0, 1)
                do(step, 1, softmax_sum, 1)
                do(step, 2, residual, 0, 1)
                do(step, 2, statistics, LNA)
                do(step, 1, softmax_bias, 1)
                do(step, 2, mean_variance, LNA)
                do(step, 2, add_eps, LNA)
                do(step, 1, gate_up, 1, 2)
                do(step, 4, statistics, LN1)
                do(step, 2, normalise, LNA)
                do(step, 3, pair_best, 0)
                do(step, 3, shift_best, 0)
                do(step, 1, mask, 1, 0)
                do(step, 1, gate_up, 1, 0)
                do(step, 2, mask_scores)
                do(step, 2, score_max)
                do(step, 3, softmax_sum, 0)
                do(step, 2, score_bias)
                do(step, 1, mask, 1, 1)
                do(step, 2, reciprocal)
                do(step, 3, softmax_bias, 0)
                do(step, 4, mean_variance, LN1)
                do(step, 1, make_dense, 1, 0)
                do(step, 2, add_attention)
                do(step, 4, add_eps, LN1)
                do(step, 1, last_row, 1, 0)
                do(step, 2, statistics, LN2)
                do(step, 2, mean_variance, LN2)
                do(step, 2, add_eps, LN2)
                do(step, 1, weigh, 1, 0)
                do(step, 1, make_dense, 1, 1)
                do(step, 1, last_row, 1, 1)
                do(step, 2, normalise, LN2)
                do(step, 1, residual, 1, 0)
                do(step, 4, normalise, LN1)

            steps(dve, run, 4)

        @block.tensor
        def _(pe):
            mm, tr = nc.tensor.matmul, nc.tensor.transpose

            def weights_of(b, name, count):
                if is_first(b):
                    pe.wait_ge(s_ld[name], count)

            def bank_free(b, order, me, release):
                last = user_before(order, b.step, me)
                if last:
                    pe.wait_ge(release(*order[last[0]][:-1]), last[1])

            def aux_free(b, s):
                bank_free(b, AUX_ORDER, [user[0] for user in AUX_ORDER].index(s), lambda s: s)

            def transpose_h(b, ln):
                if is_first(b) and ln == LN1:
                    return
                pe.wait_ge(s_hn[ln], b.after)
                aux_free(b, s_hT[ln])
                for j in range(NJ):
                    ins = tr(bank[AUX][:, j * P:(j + 1) * P], hn[:, ln, j], ident[:, :])
                ins.then_inc(s_hTp[ln], 1)

            def similarities(b, s, j):
                ln = (LN1, LN2)[s]
                pe.wait_ge(s_hT[ln], b.after)
                bank_free(b, SIM_ORDER[j], place(SIM_ORDER[j], s), lambda s: s_sim[s][j])
                mm(bank[SIM + j][:, :], hT[:, ln, j * P:(j + 1) * P], router[:, :], start=True,
                   stop=True).then_inc(s_simp[s][j], 1)
                if is_first(b) and (s, j) == (0, 1):
                    pe.wait_ge(s_trc[2], 2)
                    mm(bank[6][:, 0:D], qwT[:, :], kwT[:, :], start=True, stop=True).then_inc(s_fold[1], 1)

            def fill(b, s, kind, c):
                ln = (LN1, LN2)[s]
                at = mlp_bank(s, kind, c)
                pe.wait_ge(s_hT[ln], b.after)
                order = MLP_ORDER[at - MLP]
                bank_free(b, order, place(order, s, kind, c), lambda s, kind, c: s_drain[s][kind][c // 2])
                w = {EXPERTS: downT, GATE: wg, UP: wu}[kind]
                weights_of(b, "mlp", 2 * 16)
                for i in range(2):
                    ins = mm(bank[at][:, i * S:(i + 1) * S], w[:, (c + i) * P:(c + i + 1) * P], hT[:, ln], start=True,
                             stop=True)
                ins.then_inc(s_fill[s][kind][c // 2], 1)

            def turn(b, s, j):
                pe.wait_ge(s_fix[s][j], b.after)
                if is_first(b):
                    pe.wait_ge(s_trc[3], 1)
                bank_free(b, ST_ORDER, place(ST_ORDER, s, j), lambda s, j: s_wT[s][j])
                for c in range(FC):
                    ins = tr(bank[ST][:, c * P:(c + 1) * P], dense[:, j, c * P:(c + 1) * P], ident[:, :])
                ins.then_inc(s_sT[s][j], 1)

            def mlp_output(b, s, j):
                bank_free(b, Y_ORDER, place(Y_ORDER, s, j), lambda s, j: s_res[s][j])
                for ready in s_drain[s][UP] if s in FUSED else [s_act[s]]:
                    pe.wait_ge(ready, b.after)
                if is_first(b):
                    pe.wait_ge(s_foldc[1], 1)
                weights_of(b, "others", 4 * 16)
                y = bank[Y][:, 0:D]
                mm(y, ones[:, :], bd[:, :], start=True, stop=False)
                for c in range(FC):
                    ins = mm(y, act[:, s, c, j * P:(j + 1) * P], wd[:, c], start=False, stop=False)
                ins.then_inc(s_ym[s][j], 1)

            def expert_output(b, s, j):
                pe.wait_ge(s_wT[s][j], b.after)
                for c in range(FC):
                    ins = mm(bank[Y][:, 0:D], wT[:, j, c], up[:, c], start=False, stop=c == FC - 1)
                ins.then_inc(s_y[s][j], 1)

            def project(b):
                pe.wait_ge(s_hT[LNA], b.after)
                aux_free(b, s_tv)
                mm(bank[AUX][:, 0:S], qk[:, :], hT[:, LNA], start=True, stop=True)
                for j in range(NJ):
                    ins = mm(bank[AUX][:, S + j * P:S + (j + 1) * P], hT[:, LNA, j * P:(j + 1) * P], vw[:, :],
                             start=True, stop=True)
                ins.then_inc(s_tvp, 1)

            def score(b):
                pe.wait_ge(s_tv, b.after)
                aux_free(b, s_sc)
                mm(bank[AUX][:, 0:P], tv[:, 0:P], hT[:, LNA, 0:P], start=True, stop=True)
                mm(bank[AUX][:, P:3 * P], tv[:, P:2 * P], hT[:, LNA], start=True, stop=True).then_inc(s_scp, 1)

            def transpose_probs(b):
                pe.wait_ge(s_pr, b.after)
                aux_free(b, s_prT)
                for k in range(3):
                    ins = tr(bank[AUX][:, k * P:(k + 1) * P], pr[:, k * P:(k + 1) * P], ident[:, :])
                ins.then_inc(s_prTp, 1)

            def attend(b):
                pe.wait_ge(s_prT, b.after)
                aux_free(b, s_x2)
                o = bank[AUX]
                mm(o[:, 0:D], prT[:, 0:P], tv[:, S:S + D], start=True, stop=True)
                mm(o[:, D:2 * D], prT[:, P:2 * P], tv[:, S:S + D], start=True, stop=False)
                mm(o[:, D:2 * D], prT[:, 2 * P:3 * P], tv[:, S + D:S + 2 * D], start=False, stop=True).then_inc(s_o, 1)

            pe.wait_ge(s_const, 5)
            pe.wait_ge(s_ld["wq"], 16)
            for g in range(2 * H):
                ins = tr(bank[g // H][0:NQ, (g % H) * D:(g % H + 1) * D], wq[:, g * NQ:(g + 1) * NQ], ident[:, :])
                if g % H == H - 1:
                    ins.then_inc(s_tr[0], 1)
            pe.wait_ge(s_ld["keys"], 16)
            for side in range(2):
                for h in range(H):
                    g = side * H + h
                    ins = tr(bank[2][0:NQ, g * NK:(g + 1) * NK], keys[:, h, side * NQ:(side + 1) * NQ],
                             ident[0:NK, 0:NK])
            ins.then_inc(s_tr[1], 1)
            pe.wait_ge(s_ld["down"], 16)
            for c in range(FC):
                ins = tr(bank[3][:, c * P:(c + 1) * P], down[:, c], ident[:, :])
            ins.then_inc(s_tr[2], 1)
            pe.wait_ge(s_trc[0], 3)
            for g in range(2 * H):
                ins = mm(bank[4][:, g * NK:(g + 1) * NK], wqT[:, g], keyT[:, g], start=True, stop=True)
            ins.then_inc(s_fold[0], 1)
            pe.wait_ge(s_hn[LN1], 1)
            for j in range(NJ):
                ins = tr(bank[AUX][:, j * P:(j + 1) * P], hn[:, LN1, j], ident[:, :])
            ins.then_inc(s_hTp[LN1], 1)
            pe.wait_ge(s_ld["qk"], 32)
            tr(bank[5][:, 0:D], qw[:, :], ident[:, :])
            tr(bank[5][:, D:2 * D], kw[:, :], ident[:, :])
            pe.wait_ge(s_ld["b"], 32)
            tr(bank[5][:, 2 * D:2 * D + 2 * FC], brow[:, :], ident[0:2 * FC, 0:2 * FC]).then_inc(s_tr[3], 1)
            pe.wait_ge(s_foldc[0], 1)
            pe.wait_ge(s_trc[1], 1)

            def run(step):
                do(step, 1, attend)
                do(step, 2, fill, 0, EXPERTS, 0)
                do(step, 0, turn, 1, 0)
                do(step, 0, expert_output, 1, 0)
                do(step, 0, turn, 1, 1)
                do(step, 1, transpose_h, LN2)
                do(step, 0, mlp_output, 1, 1)
                do(step, 3, transpose_h, LN1)
                do(step, 1, similarities, 1, 0)
                do(step, 0, expert_output, 1, 1)
                do(step, 1, similarities, 1, 1)
                do(step, 2, mlp_output, 0, 0)
                do(step, 3, similarities, 0, 0)
                do(step, 3, similarities, 0, 1)
                do(step, 1, fill, 1, EXPERTS, 0)
                do(step, 1, fill, 1, GATE, 2)
                do(step, 2, turn, 0, 0)
                do(step, 1, fill, 1, GATE, 0)
                do(step, 3, fill, 0, GATE, 0)
                do(step, 2, expert_output, 0, 0)
                do(step, 3, fill, 0, GATE, 2)
                do(step, 2, turn, 0, 1)
                do(step, 2, mlp_output, 0, 1)
                do(step, 2, expert_output, 0, 1)
                do(step, 1, fill, 1, UP, 2)
                do(step, 1, fill, 1, UP, 0)
                do(step, 3, fill, 0, UP, 2)
                do(step, 2, transpose_h, LNA)
                do(step, 3, fill, 0, UP, 0)
                do(step, 2, project)
                do(step, 2, score)
                do(step, 1, fill, 1, EXPERTS, 2)
                do(step, 3, fill, 0, EXPERTS, 2)
                do(step, 2, transpose_probs)
                do(step, 1, mlp_output, 1, 0)

            steps(pe, run, 3)


_INS = ["L0_attn_x", "L0_attn_Qw", "L0_attn_Kw", "L0_attn_Vw", "L0_ffn_Wg", "L0_ffn_bg", "L0_ffn_Wu", "L0_ffn_bu",
        "L0_ffn_Wd", "L0_ffn_bd", "L0_ffn_Wq", "L0_ffn_keys", "L0_ffn_down_embed", "L0_ffn_up_embed"]


def kernel(**inputs):
    import concourse.bacc as bacc
    from concourse.bass_utils import run_bass_kernel_spmd

    nc = bacc.Bacc("TRN2", target_bir_lowering=False, num_devices=1)
    arrays, args = {}, []
    for name in _INS:
        a = np.ascontiguousarray(inputs[name])
        arrays["in_" + name] = a
        args.append(nc.dram_tensor("in_" + name, a.shape, mybir.dt.from_np(a.dtype), kind="ExternalInput").ap())
    args.append(nc.dram_tensor("out_x", (B, S, D), mybir.dt.float32, kind="ExternalOutput").ap())
    build(nc, *args)
    r = run_bass_kernel_spmd(nc, [arrays], core_ids=[0])
    return r.results[0]["out_x"]
```
